# Optimizing a Trainium2 kernel written in Bass

```python
import numpy as np
import jax
import jax.numpy as jnp

def _softmax(x, axis=-1):
    return jax.nn.softmax(x, axis=axis)

def _gelu(x):
    return jax.nn.gelu(x, approximate=True)

def _silu(x):
    return jax.nn.silu(x)

def _sigmoid(x):
    return jax.nn.sigmoid(x)

def _layernorm(x, axis=-1, eps=1e-05):
    m = jnp.mean(x, axis=axis, keepdims=True)
    v = jnp.var(x, axis=axis, keepdims=True)
    return (x - m) / jnp.sqrt(v + eps)

def _scatter_add(tgt, idx, src, axis=0):
    return tgt.at[idx].add(src)

def _segment_sum(src, seg, n):
    return jax.ops.segment_sum(src, seg, n)
kernel_name = 'mk_adaln_d2_jaxref_r4_e6983a'

def setup_inputs(seed: int=0):
    np.random.seed(seed)
    _w = jnp.asarray

    def _L0_attn_setup():
        import jax, jax.numpy as jnp
        import numpy as np
        NUM_HEADS = 16
        D_MODEL = 256

        def _alibi_slopes(num_heads):
            base = (2.0 ** 8) ** (1.0 / num_heads)
            return jnp.asarray([1.0 / base ** (i + 1) for i in range(num_heads)], dtype=jnp.float32)
        key = jax.random.key(seed)
        k1, k2 = jax.random.split(key)
        x = jax.random.normal(k1, (4, 512, D_MODEL), dtype=jnp.float32)
        W_kqv = jax.random.normal(k2, (D_MODEL, 3 * D_MODEL), dtype=jnp.float32) * D_MODEL ** (-0.5)
        return {'x': x, 'W_kqv': W_kqv}
    _L0_attn_in = _L0_attn_setup()

    def _L0_ffn_setup():
        import jax, jax.numpy as jnp
        import numpy as np
        E, K, NG, TG = (64, 8, 8, 4)
        CAP = 256
        SCALE = 2.5

        def _route(x_flat, gate_weight, e_bias):
            T = x_flat.shape[0]
            logits = x_flat.astype(jnp.float32) @ gate_weight.astype(jnp.float32).T
            scores = jax.nn.sigmoid(logits)
            sfc = scores + e_bias[None, :]
            group_scores = jax.lax.top_k(sfc.reshape(T, NG, E // NG), 2)[0].sum(-1)
            _, gidx = jax.lax.top_k(group_scores, TG)
            gmask = jnp.zeros((T, NG), jnp.float32).at[jnp.arange(T)[:, None], gidx].set(1.0)
            smask = jnp.repeat(gmask, E // NG, axis=1)
            tmp = jnp.where(smask > 0, sfc, 0.0)
            _, topk_idx = jax.lax.top_k(tmp, K)
            topk_w = jnp.take_along_axis(scores, topk_idx, axis=1)
            topk_w = topk_w / (topk_w.sum(-1, keepdims=True) + 1e-20)
            return (topk_idx, topk_w * SCALE)

        def _moe_forward(hidden_states, gate_weight, e_bias, w1, w2, w3, shared_gate, shared_up, shared_down):
            B, S, H = hidden_states.shape
            T = B * S
            x = hidden_states.reshape(T, H)
            topk_idx, topk_w = _route(x, gate_weight, e_bias)
            Sk = T * K
            flat_e = topk_idx.reshape(-1)
            order = jnp.argsort(flat_e)
            sorted_e = flat_e[order]
            counts = jax.ops.segment_sum(jnp.ones((Sk,), jnp.int32), flat_e, num_segments=E)
            offsets = jnp.cumsum(counts) - counts
            pos = jnp.arange(Sk) - offsets[sorted_e]
            tok_sorted = x[order // K]
            xe = jnp.zeros((E, CAP, H), x.dtype).at[sorted_e, pos].set(tok_sorted, mode='drop')
            h = jax.nn.silu(jnp.einsum('ech,efh->ecf', xe, w1)) * jnp.einsum('ech,efh->ecf', xe, w3)
            ye = jnp.einsum('ecf,ehf->ech', h, w2)
            pos_c = jnp.minimum(pos, CAP - 1)
            vals = ye[sorted_e, pos_c]
            vals = jnp.where((pos < CAP)[:, None], vals, 0.0)
            flat_w = topk_w.reshape(-1)[order].astype(vals.dtype)
            flat_t = (jnp.arange(Sk) // K)[order]
            out = jax.ops.segment_sum(vals * flat_w[:, None], flat_t, num_segments=T)
            shared = jax.nn.silu(x @ shared_gate.T) * (x @ shared_up.T) @ shared_down.T
            return (out + shared).reshape(B, S, H)
        key = jax.random.key(seed)
        ks = jax.random.split(key, 9)
        B, S, H, F = (1, 512, 256, 128)
        bound = 1.0 / 32.0
        return {'hidden_states': jax.random.normal(ks[0], (B, S, H), jnp.float32), 'gate_weight': jax.random.uniform(ks[1], (E, H), jnp.float32, -bound, bound), 'e_bias': jnp.zeros((E,), jnp.float32), 'w1': jax.random.normal(ks[2], (E, F, H), jnp.float32) * 0.02, 'w2': jax.random.normal(ks[3], (E, H, F), jnp.float32) * 0.02, 'w3': jax.random.normal(ks[4], (E, F, H), jnp.float32) * 0.02, 'shared_gate': jax.random.normal(ks[5], (2 * F, H), jnp.float32) * 0.02, 'shared_up': jax.random.normal(ks[6], (2 * F, H), jnp.float32) * 0.02, 'shared_down': jax.random.normal(ks[7], (H, 2 * F), jnp.float32) * 0.02}
    _L0_ffn_in = _L0_ffn_setup()
    _L0_c = _w((lambda *s: np.random.randn(*s).astype(np.float32) * 0.05)(1, 256))
    _L0_wmod = _w((lambda *s: np.random.randn(*s).astype(np.float32) * 0.05)(256, 6 * 256) * 256 ** (-0.5))

    def _L1_attn_setup():
        import jax, jax.numpy as jnp
        import numpy as np
        D_MODEL = 256
        N_HEADS = 16
        HEAD_D = D_MODEL // N_HEADS
        B, T = (4, 1024)
        ROPE_BASE = 10000.0

        def _rope(x):
            Bx, Tx, Dx = x.shape
            half = Dx // 2
            inv_freq = 1.0 / ROPE_BASE ** (jnp.arange(half, dtype=jnp.float32) / half)
            ang = jnp.arange(Tx, dtype=jnp.float32)[:, None] * inv_freq[None, :]
            cos, sin = (jnp.cos(ang), jnp.sin(ang))
            x1 = x[..., 0::2]
            x2 = x[..., 1::2]
            r1 = x1 * cos - x2 * sin
            r2 = x1 * sin + x2 * cos
            out = jnp.stack([r1, r2], axis=-1).reshape(Bx, Tx, Dx)
            return out
        key = jax.random.key(seed)
        k_x, k_q, k_k, k_v = jax.random.split(key, 4)
        x = jax.random.normal(k_x, (B, T, D_MODEL), dtype=jnp.float32)
        bound = np.sqrt(6.0 / (HEAD_D * N_HEADS))
        shp = (HEAD_D, HEAD_D, N_HEADS)
        w_q = jax.random.uniform(k_q, shp, jnp.float32, -bound, bound)
        w_k = jax.random.uniform(k_k, shp, jnp.float32, -bound, bound)
        w_v = jax.random.uniform(k_v, shp, jnp.float32, -bound, bound)
        return {'x': x, 'w_q': w_q, 'w_k': w_k, 'w_v': w_v}
    _L1_attn_in = _L1_attn_setup()

    def _L1_ffn_setup():
        import jax, jax.numpy as jnp
        import numpy as np
        from jax import lax
        H, DK, DV, N_EXP, CHUNK = (8, 64, 64, 4, 64)
        LORA, GATE_LR = (64, 16)
        NORMALIZER = 16.0
        EPS = 1e-05

        def chunk_gla(q, k, v, gk, C=CHUNK):
            L, h, dk = q.shape
            dv = v.shape[-1]
            nc = L // C
            qc, kc, vc, gc = (t.reshape(nc, C, h, -1) for t in (q, k, v, gk))
            g = jnp.cumsum(gc, axis=1)
            g_last = g[:, -1]
            qg = qc * jnp.exp(g)
            kg = kc * jnp.exp(-g)
            A = jnp.einsum('cthd,cshd->chts', qg, kg)
            A = A * jnp.tril(jnp.ones((C, C), q.dtype))
            o_intra = jnp.einsum('chts,cshe->cthe', A, vc)
            k_out = kc * jnp.exp(g_last[:, None] - g)
            chunk_kv = jnp.einsum('cthd,cthe->chde', k_out, vc)
            decay = jnp.exp(g_last)

            def step(S, inp):
                kv, dec, qg_c = inp
                o_inter = jnp.einsum('thd,hde->the', qg_c, S)
                return (S * dec[..., None] + kv, o_inter)
            S0 = jnp.zeros((h, dk, dv), q.dtype)
            _, o_inter = lax.scan(step, S0, (chunk_kv, decay, qg))
            return (o_intra + o_inter).reshape(L, h, dv)
        key = jax.random.key(seed)
        ks = jax.random.split(key, 20)
        B, L, Dh = (1, 1024, 256)
        KD, VD = (H * DK, H * DV)
        w = lambda i, shape: jax.random.normal(ks[i], shape, jnp.float32) * 0.02
        return {'x': jax.random.normal(ks[0], (B, L, Dh), jnp.float32), 'Wq': w(1, (Dh, KD)), 'Wk': w(2, (Dh, KD)), 'Wv': w(3, (Dh, VD)), 'Wqa': w(4, (Dh, LORA)), 'Wqb': w(5, (LORA, KD)), 'Wka': w(6, (Dh, LORA)), 'Wkb': w(7, (LORA, KD)), 'Wg1a': w(8, (Dh, GATE_LR)), 'Wg1b': w(9, (GATE_LR, KD)), 'bg1': jnp.zeros((KD,), jnp.float32), 'Wg2a': w(10, (Dh, GATE_LR)), 'Wg2b': w(11, (GATE_LR, KD)), 'bg2': jnp.zeros((KD,), jnp.float32), 'We': w(12, (Dh, N_EXP)), 'Wga': w(13, (Dh, LORA)), 'Wgb': w(14, (LORA, VD)), 'norm_w': jnp.ones((DV,), jnp.float32), 'Wo': w(15, (VD, Dh))}
    _L1_ffn_in = _L1_ffn_setup()
    _L1_c = _w((lambda *s: np.random.randn(*s).astype(np.float32) * 0.05)(1, 256))
    _L1_wmod = _w((lambda *s: np.random.randn(*s).astype(np.float32) * 0.05)(256, 6 * 256) * 256 ** (-0.5))
    _d = {'L0_attn_x': _L0_attn_in['x'], 'L0_attn_W_kqv': _L0_attn_in['W_kqv'], 'L0_ffn_gate_weight': _L0_ffn_in['gate_weight'], 'L0_ffn_e_bias': _L0_ffn_in['e_bias'], 'L0_ffn_w1': _L0_ffn_in['w1'], 'L0_ffn_w2': _L0_ffn_in['w2'], 'L0_ffn_w3': _L0_ffn_in['w3'], 'L0_ffn_shared_gate': _L0_ffn_in['shared_gate'], 'L0_ffn_shared_up': _L0_ffn_in['shared_up'], 'L0_ffn_shared_down': _L0_ffn_in['shared_down'], 'L0_c': _L0_c, 'L0_wmod': _L0_wmod, 'L1_attn_w_q': _L1_attn_in['w_q'], 'L1_attn_w_k': _L1_attn_in['w_k'], 'L1_attn_w_v': _L1_attn_in['w_v'], 'L1_ffn_Wq': _L1_ffn_in['Wq'], 'L1_ffn_Wk': _L1_ffn_in['Wk'], 'L1_ffn_Wv': _L1_ffn_in['Wv'], 'L1_ffn_Wqa': _L1_ffn_in['Wqa'], 'L1_ffn_Wqb': _L1_ffn_in['Wqb'], 'L1_ffn_Wka': _L1_ffn_in['Wka'], 'L1_ffn_Wkb': _L1_ffn_in['Wkb'], 'L1_ffn_Wg1a': _L1_ffn_in['Wg1a'], 'L1_ffn_Wg1b': _L1_ffn_in['Wg1b'], 'L1_ffn_bg1': _L1_ffn_in['bg1'], 'L1_ffn_Wg2a': _L1_ffn_in['Wg2a'], 'L1_ffn_Wg2b': _L1_ffn_in['Wg2b'], 'L1_ffn_bg2': _L1_ffn_in['bg2'], 'L1_ffn_We': _L1_ffn_in['We'], 'L1_ffn_Wga': _L1_ffn_in['Wga'], 'L1_ffn_Wgb': _L1_ffn_in['Wgb'], 'L1_ffn_norm_w': _L1_ffn_in['norm_w'], 'L1_ffn_Wo': _L1_ffn_in['Wo'], 'L1_c': _L1_c, 'L1_wmod': _L1_wmod}
    _x0 = _d['L0_attn_x']
    _d['L0_attn_x'] = jax.random.normal(jax.random.fold_in(jax.random.key(seed), 1), (1, 4096, 256), dtype=_x0.dtype)
    del _x0
    return _d

def reference(L0_attn_x, L0_attn_W_kqv, L0_ffn_gate_weight, L0_ffn_e_bias, L0_ffn_w1, L0_ffn_w2, L0_ffn_w3, L0_ffn_shared_gate, L0_ffn_shared_up, L0_ffn_shared_down, L0_c, L0_wmod, L1_attn_w_q, L1_attn_w_k, L1_attn_w_v, L1_ffn_Wq, L1_ffn_Wk, L1_ffn_Wv, L1_ffn_Wqa, L1_ffn_Wqb, L1_ffn_Wka, L1_ffn_Wkb, L1_ffn_Wg1a, L1_ffn_Wg1b, L1_ffn_bg1, L1_ffn_Wg2a, L1_ffn_Wg2b, L1_ffn_bg2, L1_ffn_We, L1_ffn_Wga, L1_ffn_Wgb, L1_ffn_norm_w, L1_ffn_Wo, L1_c, L1_wmod):

    def _L0_attn_ref(x, W_kqv):
        import jax, jax.numpy as jnp
        import numpy as np
        NUM_HEADS = 16
        D_MODEL = 256

        def _alibi_slopes(num_heads):
            base = (2.0 ** 8) ** (1.0 / num_heads)
            return jnp.asarray([1.0 / base ** (i + 1) for i in range(num_heads)], dtype=jnp.float32)
        B, S, D = x.shape
        H = NUM_HEADS
        hd = D // H
        scale = jnp.sqrt(jnp.float32(D))
        kqv = x @ W_kqv
        k, q, v = jnp.split(kqv, 3, axis=-1)
        q = q.reshape(B, S, H, hd).transpose(0, 2, 1, 3)
        k = k.reshape(B, S, H, hd).transpose(0, 2, 1, 3)
        v = v.reshape(B, S, H, hd).transpose(0, 2, 1, 3)
        pos = jnp.arange(S)
        rel = (pos[None, :] - pos[:, None]).astype(jnp.float32)
        m = _alibi_slopes(H)
        bias = m[:, None, None] * rel
        score = jnp.einsum('bhsd,bhnd->bhsn', q, k) / scale + bias[None]
        attn = jax.nn.softmax(score, axis=-1)
        out = jnp.einsum('bhsn,bhnd->bhsd', attn, v)
        out = out.transpose(0, 2, 1, 3).reshape(B, S, D)
        return out

    def _L0_ffn_ref(hidden_states, gate_weight, e_bias, w1, w2, w3, shared_gate, shared_up, shared_down):
        import jax, jax.numpy as jnp
        import numpy as np
        E, K, NG, TG = (64, 8, 8, 4)
        CAP = 256
        SCALE = 2.5

        def _route(x_flat, gate_weight, e_bias):
            T = x_flat.shape[0]
            logits = x_flat.astype(jnp.float32) @ gate_weight.astype(jnp.float32).T
            scores = jax.nn.sigmoid(logits)
            sfc = scores + e_bias[None, :]
            group_scores = jax.lax.top_k(sfc.reshape(T, NG, E // NG), 2)[0].sum(-1)
            _, gidx = jax.lax.top_k(group_scores, TG)
            gmask = jnp.zeros((T, NG), jnp.float32).at[jnp.arange(T)[:, None], gidx].set(1.0)
            smask = jnp.repeat(gmask, E // NG, axis=1)
            tmp = jnp.where(smask > 0, sfc, 0.0)
            _, topk_idx = jax.lax.top_k(tmp, K)
            topk_w = jnp.take_along_axis(scores, topk_idx, axis=1)
            topk_w = topk_w / (topk_w.sum(-1, keepdims=True) + 1e-20)
            return (topk_idx, topk_w * SCALE)

        def _moe_forward(hidden_states, gate_weight, e_bias, w1, w2, w3, shared_gate, shared_up, shared_down):
            B, S, H = hidden_states.shape
            T = B * S
            x = hidden_states.reshape(T, H)
            topk_idx, topk_w = _route(x, gate_weight, e_bias)
            Sk = T * K
            flat_e = topk_idx.reshape(-1)
            order = jnp.argsort(flat_e)
            sorted_e = flat_e[order]
            counts = jax.ops.segment_sum(jnp.ones((Sk,), jnp.int32), flat_e, num_segments=E)
            offsets = jnp.cumsum(counts) - counts
            pos = jnp.arange(Sk) - offsets[sorted_e]
            tok_sorted = x[order // K]
            xe = jnp.zeros((E, CAP, H), x.dtype).at[sorted_e, pos].set(tok_sorted, mode='drop')
            h = jax.nn.silu(jnp.einsum('ech,efh->ecf', xe, w1)) * jnp.einsum('ech,efh->ecf', xe, w3)
            ye = jnp.einsum('ecf,ehf->ech', h, w2)
            pos_c = jnp.minimum(pos, CAP - 1)
            vals = ye[sorted_e, pos_c]
            vals = jnp.where((pos < CAP)[:, None], vals, 0.0)
            flat_w = topk_w.reshape(-1)[order].astype(vals.dtype)
            flat_t = (jnp.arange(Sk) // K)[order]
            out = jax.ops.segment_sum(vals * flat_w[:, None], flat_t, num_segments=T)
            shared = jax.nn.silu(x @ shared_gate.T) * (x @ shared_up.T) @ shared_down.T
            return (out + shared).reshape(B, S, H)
        return _moe_forward(hidden_states, gate_weight, e_bias, w1, w2, w3, shared_gate, shared_up, shared_down)

    def _L1_attn_ref(x, w_q, w_k, w_v):
        import jax, jax.numpy as jnp
        import numpy as np
        D_MODEL = 256
        N_HEADS = 16
        HEAD_D = D_MODEL // N_HEADS
        B, T = (4, 1024)
        ROPE_BASE = 10000.0

        def _rope(x):
            Bx, Tx, Dx = x.shape
            half = Dx // 2
            inv_freq = 1.0 / ROPE_BASE ** (jnp.arange(half, dtype=jnp.float32) / half)
            ang = jnp.arange(Tx, dtype=jnp.float32)[:, None] * inv_freq[None, :]
            cos, sin = (jnp.cos(ang), jnp.sin(ang))
            x1 = x[..., 0::2]
            x2 = x[..., 1::2]
            r1 = x1 * cos - x2 * sin
            r2 = x1 * sin + x2 * cos
            out = jnp.stack([r1, r2], axis=-1).reshape(Bx, Tx, Dx)
            return out
        Bx, Tx, Dx = x.shape
        d = Dx // N_HEADS
        xh = x.reshape(Bx, Tx, d, N_HEADS)
        q = jnp.einsum('btqh,qdh->btdh', xh, w_q).reshape(Bx, Tx, Dx)
        k = jnp.einsum('btkh,kdh->btdh', xh, w_k).reshape(Bx, Tx, Dx)
        v = jnp.einsum('btvh,vdh->btdh', xh, w_v).reshape(Bx, Tx, Dx)
        q = _rope(q)
        k = _rope(k)
        gamma = 1.0 / jnp.sqrt(jnp.float32(Dx))
        scores = jnp.einsum('bqd,bkd->bqk', q, k) * gamma
        causal = jnp.tril(jnp.ones((Tx, Tx), dtype=bool))
        scores = jnp.where(causal[None], scores, -jnp.inf)
        attn = jax.nn.softmax(scores, axis=-1)
        y = jnp.einsum('bqt,btd->bqd', attn, v)
        return y

    def _L1_ffn_ref(x, Wq, Wk, Wv, Wqa, Wqb, Wka, Wkb, Wg1a, Wg1b, bg1, Wg2a, Wg2b, bg2, We, Wga, Wgb, norm_w, Wo):
        import jax, jax.numpy as jnp
        import numpy as np
        from jax import lax
        H, DK, DV, N_EXP, CHUNK = (8, 64, 64, 4, 64)
        LORA, GATE_LR = (64, 16)
        NORMALIZER = 16.0
        EPS = 1e-05

        def chunk_gla(q, k, v, gk, C=CHUNK):
            L, h, dk = q.shape
            dv = v.shape[-1]
            nc = L // C
            qc, kc, vc, gc = (t.reshape(nc, C, h, -1) for t in (q, k, v, gk))
            g = jnp.cumsum(gc, axis=1)
            g_last = g[:, -1]
            qg = qc * jnp.exp(g)
            kg = kc * jnp.exp(-g)
            A = jnp.einsum('cthd,cshd->chts', qg, kg)
            A = A * jnp.tril(jnp.ones((C, C), q.dtype))
            o_intra = jnp.einsum('chts,cshe->cthe', A, vc)
            k_out = kc * jnp.exp(g_last[:, None] - g)
            chunk_kv = jnp.einsum('cthd,cthe->chde', k_out, vc)
            decay = jnp.exp(g_last)

            def step(S, inp):
                kv, dec, qg_c = inp
                o_inter = jnp.einsum('thd,hde->the', qg_c, S)
                return (S * dec[..., None] + kv, o_inter)
            S0 = jnp.zeros((h, dk, dv), q.dtype)
            _, o_inter = lax.scan(step, S0, (chunk_kv, decay, qg))
            return (o_intra + o_inter).reshape(L, h, dv)
        B, L, Dh = x.shape
        scale = DK ** (-0.5)
        q1 = (x @ Wq).reshape(B, L, H, DK) * scale
        k1 = (x @ Wk).reshape(B, L, H, DK)
        v = (x @ Wv).reshape(B, L, H, DV)
        q2 = (x @ Wqa @ Wqb).reshape(B, L, H, DK) * scale
        k2 = jax.nn.softmax((x @ Wka @ Wkb).reshape(B, L, H, DK), axis=-1)
        gk1 = (jax.nn.log_sigmoid(x @ Wg1a @ Wg1b + bg1) / NORMALIZER).reshape(B, L, H, DK)
        gk2 = (jax.nn.log_sigmoid(x @ Wg2a @ Wg2b + bg2) / NORMALIZER).reshape(B, L, H, DK)
        e = jax.nn.softmax(x @ We, axis=-1)
        _, idx = lax.top_k(e, 1)
        mask = jax.nn.one_hot(idx, N_EXP, dtype=x.dtype).sum(-2)
        rw = e * mask
        fac = jnp.swapaxes(rw, 1, 2)[:, :, :, None, None]
        mfac = jnp.swapaxes(mask, 1, 2)[:, :, :, None, None]
        q_e = q2[:, None] * fac
        k_e = k2[:, None] * fac
        gk_e = gk2[:, None] * mfac
        gla_b = jax.vmap(chunk_gla)
        o_dense = gla_b(q1, k1, v, gk1)
        gla_be = jax.vmap(jax.vmap(chunk_gla, in_axes=(0, 0, None, 0)))
        o_sparse = gla_be(q_e, k_e, v, gk_e).sum(axis=1)
        o = o_dense + o_sparse
        g = (x @ Wga @ Wgb).reshape(B, L, H, DV)
        o = o * lax.rsqrt(jnp.mean(o * o, axis=-1, keepdims=True) + EPS) * norm_w
        o = o * (g * jax.nn.sigmoid(g))
        return o.reshape(B, L, H * DV) @ Wo
    x = L0_attn_x
    mod = (_silu(L0_c) @ L0_wmod).reshape(L0_c.shape[0], 6, 1, -1)
    sa, ca, ga, sb, cb, gb = (mod[:, 0], mod[:, 1], mod[:, 2], mod[:, 3], mod[:, 4], mod[:, 5])
    ga = (2 * (ga >= 0) - 1) * jnp.maximum(jnp.abs(ga), 0.25)
    gb = (2 * (gb >= 0) - 1) * jnp.maximum(jnp.abs(gb), 0.25)
    h = _layernorm(x, axis=-1) * (1 + ca) + sa
    x = x + ga * _L0_attn_ref(h, L0_attn_W_kqv)
    h = _layernorm(x, axis=-1) * (1 + cb) + sb
    x = x + gb * _L0_ffn_ref(h, L0_ffn_gate_weight, L0_ffn_e_bias, L0_ffn_w1, L0_ffn_w2, L0_ffn_w3, L0_ffn_shared_gate, L0_ffn_shared_up, L0_ffn_shared_down)
    mod = (_silu(L1_c) @ L1_wmod).reshape(L1_c.shape[0], 6, 1, -1)
    sa, ca, ga, sb, cb, gb = (mod[:, 0], mod[:, 1], mod[:, 2], mod[:, 3], mod[:, 4], mod[:, 5])
    ga = (2 * (ga >= 0) - 1) * jnp.maximum(jnp.abs(ga), 0.25)
    gb = (2 * (gb >= 0) - 1) * jnp.maximum(jnp.abs(gb), 0.25)
    h = _layernorm(x, axis=-1) * (1 + ca) + sa
    x = x + ga * _L1_attn_ref(h, L1_attn_w_q, L1_attn_w_k, L1_attn_w_v)
    h = _layernorm(x, axis=-1) * (1 + cb) + sb
    x = x + gb * _L1_ffn_ref(h, L1_ffn_Wq, L1_ffn_Wk, L1_ffn_Wv, L1_ffn_Wqa, L1_ffn_Wqb, L1_ffn_Wka, L1_ffn_Wkb, L1_ffn_Wg1a, L1_ffn_Wg1b, L1_ffn_bg1, L1_ffn_Wg2a, L1_ffn_Wg2b, L1_ffn_bg2, L1_ffn_We, L1_ffn_Wga, L1_ffn_Wgb, L1_ffn_norm_w, L1_ffn_Wo)
    return x

_drawn_inputs = setup_inputs


def setup_inputs(seed=0):
    import zlib

    import numpy as np

    out = dict(_drawn_inputs(seed))
    spreads = {'L0_ffn_e_bias': (0.0, 0.8),
     'L1_ffn_bg1': (0.0, 0.8),
     'L1_ffn_bg2': (0.0, 0.8),
     'L1_ffn_norm_w': (1.0, 0.6)}
    factors = {'L0_ffn_gate_weight': 8.0,
     'L0_ffn_w1': 8.0,
     'L0_ffn_w2': 8.0,
     'L0_ffn_w3': 8.0,
     'L0_ffn_shared_gate': 8.0,
     'L0_ffn_shared_up': 8.0,
     'L0_ffn_shared_down': 8.0,
     'L1_attn_w_q': 8.0,
     'L1_attn_w_k': 8.0,
     'L1_attn_w_v': 8.0,
     'L1_ffn_Wq': 8.0,
     'L1_ffn_Wk': 8.0,
     'L1_ffn_Wv': 8.0,
     'L1_ffn_Wqa': 8.0,
     'L1_ffn_Wqb': 8.0,
     'L1_ffn_Wka': 8.0,
     'L1_ffn_Wkb': 8.0,
     'L1_ffn_Wg1a': 8.0,
     'L1_ffn_Wg1b': 8.0,
     'L1_ffn_Wg2a': 8.0,
     'L1_ffn_Wg2b': 8.0,
     'L1_ffn_We': 8.0,
     'L1_ffn_Wga': 8.0,
     'L1_ffn_Wgb': 8.0,
     'L1_ffn_Wo': 8.0,
     'L1_c': 8.0,
     'L1_wmod': 8.0}
    for name, (base, spread) in spreads.items():
        noise = np.random.default_rng([zlib.crc32(name.encode()), seed]).standard_normal(out[name].shape)
        drawn = base * np.exp(spread * noise) if base else spread * noise
        out[name] = jnp.asarray(drawn.astype(out[name].dtype))
    for name, factor in factors.items():
        out[name] = (out[name] * factor).astype(out[name].dtype)
    return out
```

```python
from contextlib import ExitStack, contextmanager

import concourse.bass as bass
from concourse import mybir

P = 128
T = 4096
D = 256
KD = D // P
NT = T // P
CH = 512
NC = T // CH
TC = CH // P
LN_EPS = 1e-5

ALU = mybir.AluOpType
ACT = mybir.ActivationFunctionType
AX = mybir.AxisListType.X
F32 = mybir.dt.float32
BF16 = mybir.dt.bfloat16
I32 = mybir.dt.int32
U32 = mybir.dt.uint32

SA, CA, GA, SB, CB, GB = range(6)


E = 64
F = 128
FS = 256
CAP = 256
TOPK = 8
NGRP, GE, TOPG = 8, 8, 4
ROUTE_SCALE = 2.5
SLOTS = E * CAP
PAY = D + E
TAKEN = -1e30
SPARE = P
CLEAR_ROWS = 8


@contextmanager
def fresh_semaphores(nc, prefix):
    taken = []

    def sem(name):
        taken.append(nc.alloc_semaphore(prefix + name))
        return taken[-1]
    yield sem
    nc.clear_and_free_semaphores(taken)
    nc.all_engine_barrier()


def hold(eng, semaphore, value, passed):
    eng.wait_ge(semaphore, value)
    eng.sem_inc(passed, 1)


def modulation(nc, mod, ident, identb, c_in, w_in):
    with ExitStack() as ctx:
        sb = lambda n, s, d=F32: ctx.enter_context(nc.sbuf_tensor("mod_" + n, s, d))
        sem = ctx.enter_context(fresh_semaphores(nc, "mod_"))
        c_col = sb("c_col", [P, 2, KD])
        c_exp = sb("c_exp", [P, 2, KD])
        c_den = sb("c_den", [P, 2, KD])
        c_inv = sb("c_inv", [P, 2, KD])
        c_silu = sb("c_silu", [P, 2, KD])
        c_wide = sb("c_wide", [P, 2, KD, P])
        ones = sb("mod_ones", [P, P])
        wmod = sb("wmod", [P, 2, KD, 6 * D])
        absg = sb("absg", [P, 2, 2, D])
        sgn = sb("sgn", [P, 2, 2, D])
        ps = [[ctx.enter_context(nc.psum_tensor(f"ps_mod{l}{n}", [P, CH], F32)) for n in range(3)] for l in range(2)]
        c_loaded, w_loaded, c_exped, ones_set, id_clear, wide_ready, mod_summed, dve_step, ident_set = (
            sem(n) for n in ("c_loaded", "w_loaded", "c_exped", "ones_set", "id_clear", "wide_ready", "mod_summed",
                             "dve_step", "ident_set"))
        with nc.Block() as block:
            @block.sync
            def _(sp):
                for l in range(2):
                    sp.dma_start(c_col[:, l, :], c_in[l]).then_inc(c_loaded, 16)
                for l in range(2):
                    sp.dma_start(wmod[:, l, :, :], w_in[l].rearrange("(k p) n -> p k n", p=P)).then_inc(w_loaded, 16)

            @block.gpsimd
            def _(pool):
                pool.memset(ident[:, :], 0.0).then_inc(id_clear, 1)
                pool.wait_ge(id_clear, 1)
                pool.affine_select(out=ident[:, :], in_=ident[:, :], compare_op=ALU.not_equal, fill=1.0, base=0,
                                   pattern=[[-1, P]], channel_multiplier=1).then_inc(id_clear, 1)
                pool.wait_ge(id_clear, 2)
                pool.tensor_copy(identb[:, :], ident[:, :]).then_inc(ident_set, 1)

            @block.scalar
            def _(act):
                act.wait_ge(c_loaded, 32)
                act.activation(c_exp[:, :, :], c_col[:, :, :], ACT.Exp, scale=-1.0).then_inc(c_exped, 1)

            @block.vector
            def _(dve):
                n = [0]

                def link(ins):
                    n[0] += 1
                    ins.then_inc(dve_step, 1)
                    dve.wait_ge(dve_step, n[0])

                dve.memset(ones[:, :], 1.0).then_inc(ones_set, 1)
                dve.wait_ge(c_exped, 1)
                link(dve.tensor_scalar_add(c_den[:, :, :], c_exp[:, :, :], 1.0))
                link(dve.reciprocal(c_inv[:, :, :], c_den[:, :, :]))
                link(dve.tensor_tensor(c_silu[:, :, :], c_col[:, :, :], c_inv[:, :, :], ALU.mult))
                dve.wait_ge(ones_set, 1)
                for l in range(2):
                    for k in range(KD):
                        dve.tensor_scalar(c_wide[:, l, k, :], ones[:, :], c_silu[:, l, k:k + 1], None,
                                          ALU.mult).then_inc(wide_ready, 1)
                for l in range(2):
                    for j in range(3):
                        dve.wait_ge(mod_summed, 3 * l + j + 1)
                        link(dve.tensor_copy(mod[l][:, 2 * j:2 * j + 2, :], ps[l][j][:, :].rearrange("p (a d) -> p a d", a=2)))
                for l in range(2):
                    gates = mod[l][:, GA::3, :]
                    link(dve.scalar_tensor_tensor(out=absg[:, l], in0=gates, scalar=-1.0, in1=gates, op0=ALU.mult,
                                                  op1=ALU.max))
                    link(dve.tensor_scalar_max(absg[:, l], absg[:, l], 0.25))
                    link(dve.tensor_scalar(sgn[:, l], gates, 0.0, 2.0, ALU.is_ge, ALU.mult))
                    link(dve.tensor_scalar_add(sgn[:, l], sgn[:, l], -1.0))
                    link(dve.tensor_tensor(gates, absg[:, l], sgn[:, l], ALU.mult))
                    scales = mod[l][:, CA::3, :]
                    link(dve.tensor_scalar_add(scales, scales, 1.0))

            @block.tensor
            def _(pe):
                pe.wait_ge(w_loaded, 32)
                pe.wait_ge(wide_ready, 4)
                for l in range(2):
                    for j in range(3):
                        for k in range(KD):
                            mm = pe.matmul(ps[l][j][:, :], c_wide[:, l, k, :], wmod[:, l, k, j * CH:(j + 1) * CH],
                                           start=(k == 0), stop=(k == KD - 1))
                        mm.then_inc(mod_summed, 1)


NPART = 3
H0 = 16
HD0 = D // H0
HG = 4
NG = H0 // HG
VW = 32
SCALE0 = 1.0 / 16.0


def norm_chunk(dve, step, passed, base, x, stats, aggr, rstd, h, scale, shift, order=lambda ap: ap, out=None):
    for j in range(TC):
        last = dve.bn_stats(stats[:, j, :], x[:, j, :])
    last.then_inc(step, 1)
    hold(dve, step, base + 1, passed)
    for j in range(TC):
        last = dve.bn_aggr(aggr[:, j, :], stats[:, j, :])
    last.then_inc(step, 1)
    dve.wait_ge(step, base + 2)
    dve.tensor_scalar_add(rstd[:, :], aggr[:, :, 1], LN_EPS).then_inc(step, 1)
    dve.wait_ge(step, base + 4)
    dve.reciprocal(rstd[:, :], rstd[:, :]).then_inc(step, 1)
    dve.wait_ge(step, base + 5)
    for j in range(TC):
        last = dve.tensor_scalar(h[:, j, :], x[:, j, :], aggr[:, j, 0:1], rstd[:, j:j + 1], ALU.subtract, ALU.mult)
    last.then_inc(step, 1)
    dve.wait_ge(step, base + 6)
    wide = lambda row: row.unsqueeze(1).to_broadcast([P, TC, D])
    dve.tensor_tensor(h[:, :, :], h[:, :, :], wide(scale), ALU.mult).then_inc(step, 1)
    dve.wait_ge(step, base + 7)
    dve.tensor_tensor(h[:, :, :] if out is None else out, order(h[:, :, :]), order(wide(shift)),
                      ALU.add).then_inc(step, 1)
    dve.wait_ge(step, base + 8)


NORM_STEPS = 8


def sqrt_chunk(act, step, base, rstd):
    act.wait_ge(step, base + 3)
    act.activation(rstd[:, :], rstd[:, :], ACT.Sqrt).then_inc(step, 1)


def chunk_pairs(body, chunks=NC):
    def go(eng):
        with eng.Fori(0, chunks // 2 - 1) as t:
            for i in range(2):
                body(2 * t + i, t, i, True)
        for i in range(2):
            body(chunks - 2 + i, chunks // 2 - 1, i, i == 0)
    return go


def project_heads(nc, xres, mod, ident, x_in, w_in, q_parts, k_parts, v_aug):
    with ExitStack() as ctx:
        sb = lambda n, s, d=F32: ctx.enter_context(nc.sbuf_tensor("proj_" + n, s, d))
        pb = lambda n, s, d=F32: ctx.enter_context(nc.psum_tensor("proj_" + n, s, d))
        sem = ctx.enter_context(fresh_semaphores(nc, "proj_"))
        w = sb("w_kqv", [P, KD, 3 * D])
        h = [sb(f"h{i}", [P, TC, D]) for i in range(2)]
        hT = [sb(f"hT{i}", [P, KD, CH]) for i in range(2)]
        stats, aggr, rstd = sb("stats", [P, TC, 6]), sb("aggr", [P, TC, 2]), sb("rstd", [P, TC])
        parts = [sb(f"parts{i}", [P, NPART, CH], BF16) for i in range(2)]
        rest = [sb(f"rest{i}", [P, CH]) for i in range(2)]
        vbuf = [sb(f"vbuf{i}", [P, TC, H0, VW]) for i in range(2)]
        psT = [pb(f"psT{k}", [P, CH]) for k in range(KD)]
        psQ = [pb(f"psQ{b}", [P, CH]) for b in range(4)]
        psV = [pb(f"psV{i}", [P, CH]) for i in range(2)]
        w_loaded = sem("w_loaded")
        x_loaded = [sem(f"x_loaded{i}") for i in range(2)]
        norm_step, hT_summed, hT_copied, dve_passed, pool_passed = (
            sem(n) for n in ("norm_step", "hT_summed", "hT_copied", "dve_passed", "pool_passed"))
        qk_summed, qk_high, qk_rest, qk_mid, qk_parts, v_set, v_summed, v_copied = (
            sem(n) for n in ("qk_summed", "qk_high", "qk_rest", "qk_mid", "qk_parts", "v_set", "v_summed", "v_copied"))
        parts_stored = [sem(f"parts_stored{i}") for i in range(2)]
        v_stored = [sem(f"v_stored{i}") for i in range(2)]
        NB = 4
        cols = [D, D + P, 0, P]
        with nc.Block() as block:
            @block.sync
            def _(sp):
                x_view = x_in.rearrange("a (n p) d -> p (a n) d", p=P)
                sp.dma_start(w[:, :, :], w_in.rearrange("(k p) n -> p k n", p=P)).then_inc(w_loaded, 16)
                with sp.Fori(0, NC // 2) as t:
                    for i in range(2):
                        sp.wait_ge(x_loaded[i], 16 * t)
                        tiles = bass.ds((2 * t + i) * TC, TC)
                        sp.dma_start(xres[:, tiles, :], x_view[:, tiles, :]).then_inc(x_loaded[i], 16)
                with sp.Fori(0, NC) as c:
                    for b in range(NB):
                        out = (q_parts if b < 2 else k_parts)[:, b % 2 * P:b % 2 * P + P, bass.ds(c * CH, CH)]
                        sp.wait_ge(qk_parts, NB * c + b + 1)
                        sp.dma_start(out.rearrange("a p n -> p a n"), parts[b % 2][:, :, :]).then_inc(parts_stored[b % 2], 16)
                for i in range(2):
                    sp.wait_ge(parts_stored[i], 16 * 2 * NC)

            @block.gpsimd
            def _(pool):
                for i in range(2):
                    pool.memset(vbuf[i][:, :, :, :], 0.0).then_inc(v_set, 1)
                pool.wait_ge(v_set, 2)
                for i in range(2):
                    pool.memset(vbuf[i][:, :, :, HD0:HD0 + 1], 1.0).then_inc(v_set, 1)
                with pool.Fori(0, NC) as c:
                    for b in range(NB):
                        hold(pool, qk_rest, NB * (c + 1) + b + 1, pool_passed)
                        pool.tensor_copy(parts[b % 2][:, 1, :], rest[b % 2][:, :]).then_inc(qk_mid, 1)
                        pool.wait_ge(qk_mid, NB * c + b + 1)
                        pool.tensor_tensor(parts[b % 2][:, 2, :], rest[b % 2][:, :], parts[b % 2][:, 1, :],
                                           ALU.subtract).then_inc(qk_parts, 1)

            @block.scalar
            def _(act):
                def copy_h(c, i):
                    for k in range(KD):
                        act.wait_ge(hT_summed, KD * (c + 1) + k + 1)
                        act.wait_ge(v_summed, 2 * c)
                        act.activation(hT[i][:, k, :], psT[k][:, :], ACT.Copy).then_inc(hT_copied, 1)

                def chunk(c, t, i, another):
                    for b in range(NB):
                        act.wait_ge(qk_summed, NB * c + b + 1)
                        act.wait_ge(parts_stored[b % 2], 16 * (2 * c + b // 2))
                        act.activation(parts[b % 2][:, 0, :], psQ[b][:, :], ACT.Copy,
                                       scale=SCALE0 if b < 2 else 1.0).then_inc(qk_high, 1)
                    if another:
                        copy_h(c + 1, 1 - i)
                    act.wait_ge(v_set, 4)
                    act.wait_ge(v_stored[i], 16 * NG * t)
                    for m in range(2):
                        act.wait_ge(v_summed, 2 * (c + 1) + m + 1)
                        act.activation(vbuf[i][:, 2 * m:2 * m + 2, :, 0:HD0],
                                       psV[m][:, :].rearrange("p (n h d) -> p n h d", n=2, h=H0),
                                       ACT.Copy).then_inc(v_copied, 1)
                    act.wait_ge(v_copied, 2 * c + 2)
                    for g in range(NG):
                        act.dma_start(v_aug[g, :, bass.ds(c * TC, TC), :],
                                      vbuf[i][:, :, HG * g:HG * g + HG, :].rearrange("p n h w -> p n (h w)")
                                      ).then_inc(v_stored[i], 16)
                    if not isinstance(c, int):
                        sqrt_chunk(act, norm_step, NORM_STEPS * (c + 2), rstd)
                sqrt_chunk(act, norm_step, 0, rstd)
                copy_h(0, 0)
                sqrt_chunk(act, norm_step, NORM_STEPS, rstd)
                chunk_pairs(chunk)(act)
                for i in range(2):
                    act.wait_ge(v_stored[i], 16 * NG * (NC // 2))

            @block.vector
            def _(dve):
                dve.sem_inc(qk_rest, NB)

                def norm(c, t, i):
                    dve.wait_ge(x_loaded[i], 16 * (t + 1))
                    dve.wait_ge(hT_summed, KD * c)
                    norm_chunk(dve, norm_step, dve_passed, NORM_STEPS * c, xres[:, bass.ds(c * TC, TC), :], stats, aggr,
                               rstd, h[i], mod[:, CA, :], mod[:, SA, :])

                def chunk(c, t, i, another):
                    for b in range(NB):
                        dve.wait_ge(qk_high, NB * c + b + 1)
                        dve.wait_ge(qk_parts, NB * c + max(b - 1, 0))
                        dve.scalar_tensor_tensor(out=rest[b % 2][:, :], in0=psQ[b][:, :],
                                                 scalar=SCALE0 if b < 2 else 1.0, in1=parts[b % 2][:, 0, :],
                                                 op0=ALU.mult, op1=ALU.subtract).then_inc(qk_rest, 1)
                    if not isinstance(c, int):
                        norm(c + 2, t + 1, i)
                norm(0, 0, 0)
                norm(1, 0, 1)
                chunk_pairs(chunk)(dve)

            @block.tensor
            def _(pe):
                pe.sem_inc(hT_summed, KD)
                pe.sem_inc(v_summed, 2)
                pe.wait_ge(w_loaded, 16)

                def turn(c, i):
                    pe.wait_ge(norm_step, NORM_STEPS * (c + 1))
                    pe.wait_ge(hT_copied, KD * c)
                    for k in range(KD):
                        for j in range(TC):
                            mm = pe.transpose(psT[k][:, j * P:(j + 1) * P], h[i][:, j, k * P:(k + 1) * P], ident[:, :])
                        mm.then_inc(hT_summed, 1)

                def chunk(c, t, i, another):
                    pe.wait_ge(hT_copied, KD * (c + 1))
                    for b in range(NB):
                        pe.wait_ge(qk_rest, NB * c + b + 1)
                        for k in range(KD):
                            mm = pe.matmul(psQ[b][:, :], w[:, k, cols[b]:cols[b] + P], hT[i][:, k, :],
                                           start=(k == 0), stop=(k == KD - 1))
                        mm.then_inc(qk_summed, 1)
                    if another:
                        turn(c + 1, 1 - i)
                    for m in range(2):
                        pe.wait_ge(v_copied, 2 * c)
                        for j in range(2):
                            for k in range(KD):
                                mm = pe.matmul(psV[m][:, j * D:(j + 1) * D], hT[i][:, k, (2 * m + j) * P:(2 * m + j + 1) * P],
                                               w[:, k, 2 * D:3 * D], start=(k == 0), stop=(k == KD - 1))
                        mm.then_inc(v_summed, 1)
                turn(0, 0)
                chunk_pairs(chunk)(pe)


KROW = [0, 1, 0, 2, 1, 0]
QROW = [0, 0, 1, 0, 1, 2]
NSLOT = len(KROW)
AUX = NSLOT * HD0
NAUX = P - AUX
BIAS = 3 * HG
STEPS = NG * NC
UNITS = TC * HG * (T // 1024)
FAST = 6
QUART = NT // 4
UNIT_TILES = (UNITS - 3 * FAST) // 2 + FAST
assert AUX % 32 == 0 and 3 * HG + 3 <= NAUX and 3 * FAST + 2 * (UNIT_TILES - FAST) == UNITS and UNIT_TILES < NT - 1


def units_of(k):
    start = lambda n: 2 * n + min((n + 3) // 5, FAST)
    return range(min(start(k), UNITS), min(start(k + 1), UNITS))


def bias_attention(nc, identb, q_parts, k_parts, v_aug, k_aux, q_aux, o_rows, x_rows, y_rows):
    with ExitStack() as ctx:
        sb = lambda n, s, d=F32: ctx.enter_context(nc.sbuf_tensor("attn_" + n, s, d))
        pb = lambda n, s, d=F32: ctx.enter_context(nc.psum_tensor("attn_" + n, s, d))
        sem = ctx.enter_context(fresh_semaphores(nc, "attn_"))
        kmax = sb("kmax", [P, HG, T], BF16)
        kexp = sb("kexp", [P, HG, T], BF16)
        vals = sb("vals", [P, NT, HG * VW])
        qmax = [sb(f"qmax{i}", [P, HG, CH], BF16) for i in range(2)]
        qexp = [sb(f"qexp{i}", [P, HG, CH], BF16) for i in range(2)]
        probs = [sb(f"probs{i}", [P, HG, CH]) for i in range(2)]
        o_sb = [sb(f"o_sb{i}", [P, CH]) for i in range(2)]
        zeros = sb("zeros", [P, CLEAR_ROWS, PAY])
        mpart = sb("mpart", [P, TC * HG, UNITS // (TC * HG)])
        mall, mrest, mrest2 = sb("mall", [P, TC, HG]), sb("mrest", [P, TC, HG]), sb("mrest2", [P, TC, HG])
        mrows = sb("mrows", [P, TC, NAUX], BF16)
        ps_max = [pb(f"ps_max{i}", [P, 2, CH]) for i in range(2)]
        ps_exp = [pb(f"ps_exp{i}", [P, CH]) for i in range(3)]
        ps_out = pb("ps_out", [P, CH])
        ps_rows = ps_max[0][:, 0, :].bitcast(BF16)[AUX:P, 0:CH]

        loads = lambda n: [sem(f"{n}{i}") for i in range(4)]
        kmax_loaded, kexp_loaded = loads("kmax_loaded"), loads("kexp_loaded")
        vals_loaded = loads("vals_loaded")
        qmax_loaded = [sem(f"qmax_loaded{i}") for i in range(2)]
        qexp_loaded = [sem(f"qexp_loaded{i}") for i in range(2)]
        max_gate, exp_gate, sp_passed = sem("max_gate"), sem("exp_gate"), sem("sp_passed")
        unit_summed, unit_read, rows_ready, rows_turned, rows_copied = (
            sem(n) for n in ("unit_summed", "unit_read", "rows_ready", "rows_turned", "rows_copied"))
        max_step, ones_set, score_ready, exp_done, pv_done, o_copied = (
            sem(n) for n in ("max_step", "ones_set", "score_ready", "exp_done", "pv_done", "o_copied"))
        o_stored = [sem(f"o_stored{i}") for i in range(2)]
        zeros_set, cleared = sem("zeros_set"), sem("cleared")
        SCORES = NT * HG
        LAST_IN_BANK = [max(n for n in range(SCORES) if n % 3 == bank) for bank in range(3)]

        with nc.Block() as block:
            @block.sync
            def _(sp):
                def load_q(buf, done, g, c):
                    for r in range(NSLOT):
                        src = q_parts[QROW[r], bass.ds(g * HG * HD0, HG * HD0), c * CH:(c + 1) * CH]
                        sp.dma_start(buf[r * HD0:(r + 1) * HD0, :, :],
                                     src.rearrange("(j d) n -> d j n", j=HG)).then_inc(done, 16)
                    sp.dma_start(buf[AUX:P, :, :], q_aux).then_inc(done, 16)

                def load_k(buf, done, g, j0, nj, n0, nn):
                    for r in range(NSLOT):
                        src = k_parts[KROW[r], bass.ds(g * HG * HD0 + j0 * HD0, nj * HD0), n0:n0 + nn]
                        sp.dma_start(buf[r * HD0:(r + 1) * HD0, j0:j0 + nj, n0:n0 + nn],
                                     src.rearrange("(j d) n -> d j n", j=nj)).then_inc(done, 16)
                    sp.dma_start(buf[AUX:P, j0:j0 + nj, n0:n0 + nn],
                                 k_aux[g, :, j0:j0 + nj, n0:n0 + nn]).then_inc(done, 16)

                LK, LQ = 16 * (NSLOT + 1), 16 * (NSLOT + 1)

                def step(g, c, first, last):
                    s = g * NC + c
                    i = c % 2
                    nxt = lambda d: (g + (c + d) // NC, (c + d) % NC)
                    if not (last and c >= NC - 2):
                        hold(sp, unit_summed, UNITS * (s + 1), sp_passed)
                        load_q(qmax[i], qmax_loaded[i], *nxt(2))
                    if not (last and c == NC - 1):
                        hold(sp, score_ready, SCORES * s, sp_passed)
                        load_q(qexp[1 - i], qexp_loaded[1 - i], *nxt(1))
                    if c == NC - 2 and not last:
                        for j in range(HG):
                            hold(sp, unit_summed, UNITS * (s + 1) + UNITS // HG * (j + 1), sp_passed)
                            load_k(kmax, kmax_loaded[j], g + 1, j, 1, 0, T)
                    if c == NC - 1 and not last:
                        for b in range(4):
                            hold(sp, score_ready, SCORES * s + HG * QUART * (b + 1), sp_passed)
                            load_k(kexp, kexp_loaded[b], g + 1, 0, HG, b * QUART * P, QUART * P)
                            hold(sp, pv_done, NT * s + QUART * (b + 1) + 2, sp_passed)
                            sp.dma_start(vals[:, b * QUART:(b + 1) * QUART, :],
                                         v_aug[g + 1, :, b * QUART:(b + 1) * QUART, :]).then_inc(vals_loaded[b], 16)
                    if not (first and c == 0):
                        store_o(*nxt(-1))

                def store_o(g, c):
                    hold(sp, o_copied, g * NC + c + 1, sp_passed)
                    sp.dma_start(o_rows[g, :, c * CH:(c + 1) * CH], o_sb[c % 2][:, :]).then_inc(o_stored[c % 2], 16)

                load_q(qmax[0], qmax_loaded[0], 0, 0)
                for j in range(HG):
                    load_k(kmax, kmax_loaded[j], 0, j, 1, 0, T)
                load_q(qmax[1], qmax_loaded[1], 0, 1)
                load_q(qexp[0], qexp_loaded[0], 0, 0)
                for b in range(4):
                    load_k(kexp, kexp_loaded[b], 0, 0, HG, b * QUART * P, QUART * P)
                    sp.dma_start(vals[:, b * QUART:(b + 1) * QUART, :],
                                 v_aug[0, :, b * QUART:(b + 1) * QUART, :]).then_inc(vals_loaded[b], 16)
                for c in range(NC):
                    step(0, c, True, False)
                with sp.Fori(1, NG - 1) as g:
                    for c in range(NC):
                        step(g, c, False, False)
                for c in range(NC):
                    step(NG - 1, c, False, True)
                store_o(NG - 1, NC - 1)
                for i in range(2):
                    sp.wait_ge(o_stored[i], 16 * STEPS // 2)

            @block.gpsimd
            def _(pool):
                LD = 16 * (NSLOT + 1)

                def max_ready(g, c):
                    hold(pool, qmax_loaded[c % 2], LD * (g * (NC // 2) + c // 2 + 1), max_gate)

                def kmax_ready(g, c):
                    for j in range(HG):
                        hold(pool, kmax_loaded[j], LD * (g + 1), max_gate)

                def exp_ready(g, c):
                    hold(pool, qexp_loaded[c % 2], LD * (g * (NC // 2) + c // 2 + 1), exp_gate)

                def kexp_ready(g, b):
                    pool.wait_ge(kexp_loaded[b], LD * (g + 1))
                    hold(pool, vals_loaded[b], 16 * (g + 1), exp_gate)

                max_ready(0, 0)
                kmax_ready(0, 0)

                pool.memset(zeros[:, :, :], 0.0).then_inc(zeros_set, 1)
                pool.wait_ge(zeros_set, 1)
                step_rows = P * CLEAR_ROWS
                for b in range(SLOTS // step_rows):
                    pool.dma_start(x_rows[b * step_rows:(b + 1) * step_rows, :].rearrange("(p r) d -> p r d", p=P),
                                   zeros[:, :, :]).then_inc(cleared, 16)
                pool.dma_start(y_rows[SLOTS:SLOTS + SPARE, :], zeros[:, 0, 0:D]).then_inc(cleared, 16)

                def step(g, c, last):
                    exp_ready(g, c)
                    for b in range(4):
                        kexp_ready(g, b)
                        if b == 0 and not (last and c == NC - 1):
                            max_ready(g + (c + 1) // NC, (c + 1) % NC)
                            kmax_ready(g + (c + 1) // NC, 0)
                with pool.Fori(0, NG - 1) as g:
                    for c in range(NC):
                        step(g, c, False)
                for c in range(NC):
                    step(NG - 1, c, True)
                pool.wait_ge(cleared, 16 * (SLOTS // step_rows + 1))

            @block.scalar
            def _(act):
                def exps(s, i, k):
                    act.wait_ge(pv_done, NT * s + k + 1)
                    for j in range(HG):
                        n = HG * k + j
                        act.wait_ge(score_ready, SCORES * s + n + 1)
                        act.activation(probs[k % 2][:, j, :], ps_exp[n % 3][:, :], ACT.Exp).then_inc(exp_done, 1)

                def copy_o(s, i):
                    act.wait_ge(o_stored[i], 8 * (s - i))
                    act.wait_ge(pv_done, NT * (s + 1) + 2)
                    act.activation(o_sb[i][:, :], ps_out[:, :], ACT.Copy).then_inc(o_copied, 1)

                def step(s, i, first):
                    exps(s, i, 0)
                    if not first:
                        copy_o(s - 1, 1 - i)
                    for k in range(1, NT):
                        exps(s, i, k)

                step(0, 0, True)
                step(1, 1, False)
                with act.Fori(1, STEPS // 2) as t:
                    for i in range(2):
                        step(2 * t + i, i, False)
                copy_o(STEPS - 1, 1)

            @block.vector
            def _(dve):
                dve.memset(mrows[:, :, :], 0.0).then_inc(ones_set, 1)
                dve.wait_ge(ones_set, 1)
                dve.memset(mrows[:, :, BIAS:BIAS + 3], 1.0).then_inc(ones_set, 1)
                part = lambda n: mrows[:, :, 0:3 * HG].rearrange("p t (j i) -> p t j i", i=3)[:, :, :, n]
                SM = 5

                def step(s, i):
                    for u in range(UNITS):
                        dve.wait_ge(unit_summed, UNITS * s + u + 1)
                        dve.tensor_reduce(mpart[:, u // 4, u % 4:u % 4 + 1], ps_max[u % 2][:, :, :],
                                          mybir.AxisListType.XY, ALU.max).then_inc(unit_read, 1)
                    dve.wait_ge(unit_read, UNITS * (s + 1) + 2)
                    dve.tensor_reduce(mall[:, :, :].rearrange("p t j -> p j t"),
                                      mpart[:, :, :].rearrange("p (j t) m -> p j t m", j=HG), AX,
                                      ALU.max).then_inc(max_step, 1)
                    dve.wait_ge(max_step, SM * s + 1)
                    dve.wait_ge(rows_turned, s)
                    dve.tensor_scalar(part(0), mall[:, :, :], -1.0, None, ALU.mult).then_inc(max_step, 1)
                    dve.wait_ge(max_step, SM * s + 2)
                    dve.scalar_tensor_tensor(out=mrest[:, :, :], in0=mall[:, :, :], scalar=-1.0, in1=part(0),
                                             op0=ALU.mult, op1=ALU.subtract).then_inc(max_step, 1)
                    dve.wait_ge(max_step, SM * s + 3)
                    dve.tensor_copy(part(1), mrest[:, :, :]).then_inc(max_step, 1)
                    dve.wait_ge(max_step, SM * s + 4)
                    dve.tensor_tensor(mrest2[:, :, :], mrest[:, :, :], part(1), ALU.subtract).then_inc(max_step, 1)
                    dve.wait_ge(max_step, SM * s + 5)
                    dve.tensor_copy(part(2), mrest2[:, :, :]).then_inc(rows_ready, 1)
                    dve.wait_ge(qexp_loaded[i], 8 * (NSLOT + 1) * (s - i + 2))
                    dve.wait_ge(rows_turned, s + 1)
                    for j in range(HG):
                        last = dve.tensor_copy(qexp[i][AUX:P, j, :], ps_rows)
                    last.then_inc(rows_copied, 1)

                with dve.Fori(0, STEPS // 2) as t:
                    for i in range(2):
                        step(2 * t + i, i)

            @block.tensor
            def _(pe):
                pe.sem_inc(unit_read, 2)
                pe.sem_inc(pv_done, 2)

                def unit(s, i, u):
                    j, rest = divmod(u, UNITS // HG)
                    tile, m = divmod(rest, 4)
                    pe.wait_ge(unit_read, UNITS * s + u + 1)
                    if u == 0:
                        pe.wait_ge(max_gate, (HG + 1) * s + 1)
                        pe.wait_ge(rows_copied, s)
                    if rest == 0:
                        pe.wait_ge(max_gate, (HG + 1) * s + 2 + j)
                    for b in range(2):
                        n0 = (2 * m + b) * CH
                        mm = pe.matmul(ps_max[u % 2][:, b, :], qmax[i][:, j, tile * P:(tile + 1) * P],
                                       kmax[:, j, n0:n0 + CH], start=True, stop=True)
                    mm.then_inc(unit_summed, 1)

                def turn_rows(s):
                    pe.wait_ge(rows_ready, s + 1)
                    for tile in range(TC):
                        mm = pe.transpose(ps_rows[:, tile * P:(tile + 1) * P], mrows[:, tile, :], identb[:, :])
                    mm.then_inc(rows_turned, 1)

                def score(s, i, k, j):
                    n = HG * k + j
                    if n >= 3:
                        pe.wait_ge(exp_done, SCORES * s + n - 2)
                    elif not (isinstance(s, int) and s == 0):
                        pe.wait_ge(exp_done, SCORES * (s - 1) + LAST_IN_BANK[n] + 1)
                    pe.matmul(ps_exp[n % 3][:, :], kexp[:, j, k * P:(k + 1) * P], qexp[i][:, j, :],
                              start=True, stop=True).then_inc(score_ready, 1)

                def products(s, k):
                    pe.wait_ge(exp_done, SCORES * s + HG * (k + 1))
                    if k == 0:
                        pe.wait_ge(o_copied, s)
                    for j in range(HG):
                        mm = pe.matmul(ps_out[j * VW:(j + 1) * VW, :], vals[:, k, j * VW:(j + 1) * VW],
                                       probs[k % 2][:, j, :], start=(k == 0), stop=(k == NT - 1))
                    mm.then_inc(pv_done, 1)

                def step(s, i, first, maxima=True):
                    for k in range(NT):
                        if k == 0:
                            pe.wait_ge(exp_gate, 5 * s + 1)
                            pe.wait_ge(rows_copied, s + 1)
                        if k % QUART == 0:
                            pe.wait_ge(exp_gate, 5 * s + 2 + k // QUART)
                        units = list(units_of(k)) if maxima else []
                        three = len(units) == 3
                        for j in range(3):
                            score(s, i, k, j)
                            if units and j == (0 if three else 2):
                                unit(s + 1, 1 - i, units.pop(0))
                        if maxima and k == NT - 2:
                            turn_rows(s + 1)
                        if k >= 1:
                            products(s, k - 1)
                        elif not first:
                            products(s - 1, NT - 1)
                        if three:
                            unit(s + 1, 1 - i, units.pop(0))
                        score(s, i, k, 3)
                        for u in units:
                            unit(s + 1, 1 - i, u)

                for u in range(UNITS):
                    unit(0, 0, u)
                turn_rows(0)
                step(0, 0, True)
                step(1, 1, False)
                with pe.Fori(1, STEPS // 2 - 1) as t:
                    for i in range(2):
                        step(2 * t + i, i, False)
                step(STEPS - 2, 0, False)
                step(STEPS - 1, 1, False, maxima=False)
                products(STEPS - 1, NT - 1)


def bias_constants():
    import numpy as np

    def rounded(a):
        bits = a.view(np.uint32)
        return ((bits + 0x7FFF + ((bits >> 16) & 1)) & np.uint32(0xFFFF0000)).view(np.float32)
    base = np.float32((2.0 ** 8) ** (1.0 / H0))
    slopes = np.array([np.float32(1.0 / base ** (i + 1)) for i in range(H0)], np.float32)
    bias = slopes[:, None] * (np.arange(T, dtype=np.float32) - np.float32(T - 1))[None, :]
    k_aux = np.zeros((NG, NAUX, HG, T), np.float32)
    q_aux = np.zeros((NAUX, HG, CH), np.float32)
    for h in range(H0):
        g, j = divmod(h, HG)
        k_aux[g, 3 * j:3 * j + 3, j, :] = 1
        rest = bias[h].copy()
        for i in range(3):
            part = rounded(rest)
            k_aux[g, BIAS + i, j, :] = part
            rest = rest - part
    q_aux[BIAS:BIAS + 3] = 1
    bits = lambda a: (a.view(np.uint32) >> 16).astype(np.uint16)
    return bits(k_aux), bits(q_aux)


class Chain:

    def __init__(self, eng, semaphore, base=0):
        self.eng, self.semaphore, self.base, self.n = eng, semaphore, base, 0

    def __call__(self, ins):
        self.n += 1
        ins.then_inc(self.semaphore, 1)
        self.eng.wait_ge(self.semaphore, self.base + self.n)


SENT_AFTER, SENT_ROUTE, SENT_SHARED = range(0, 9), range(9, 13), range(13, NT)


def scatter_rows(pool, tiles, pay, slots, x_rows, done):
    for n in tiles:
        for k in range(TOPK):
            pool.indirect_dma_start(out=x_rows, out_offset=bass.IndirectOffsetOnAxis(
                ap=slots[:, n, k:k + 1].bitcast(U32), axis=0), in_=pay[:, n, :], in_offset=None,
                bounds_check=SLOTS - 1, oob_is_err=False).then_inc(done, 16)


def after_attention(nc, half, xres, pay, slots, scores, mod, ident, o_rows, w_router, x_rows):
    with ExitStack() as ctx:
        sb = lambda n, s, d=F32: ctx.enter_context(nc.sbuf_tensor(f"post{half}_" + n, s, d))
        pb = lambda n, s, d=F32: ctx.enter_context(nc.psum_tensor(f"post{half}_" + n, s, d))
        sem = ctx.enter_context(fresh_semaphores(nc, f"post{half}_"))
        wr = sb("wr", [P, KD, E])
        o_in = [sb(f"o_in{i}", [P, NG, CH]) for i in range(2)]
        o_tok = sb("o_tok", [P, TC, D])
        rden = sb("rden", [P, TC, H0])
        c0, chunks = half * NC // 2, NC // 2
        h = sb("h", [P, TC, D])
        hT = sb("hT", [P, KD, CH])
        stats, aggr, rstd = sb("stats", [P, TC, 6]), sb("aggr", [P, TC, 2]), sb("rstd", [P, TC])
        r_exp = sb("r_exp", [P, TC, E])
        psO = [pb(f"psO{j}", [P, CH]) for j in range(TC)]
        psT = [pb(f"psT{k}", [P, CH]) for k in range(KD)]
        psR = pb("psR", [P, TC, E])
        o_loaded = [sem(f"o_loaded{i}") for i in range(2)]
        (w_loaded, sp_passed, dve_passed, o_turned, o_read, x_step, norm_step, hT_summed, hT_copied,
         r_summed, r_exped, r_step, r_read, pay_copied, scattered) = (
            sem(n) for n in ("w_loaded", "sp_passed", "dve_passed", "o_turned", "o_read", "x_step", "norm_step",
                             "hT_summed", "hT_copied", "r_summed", "r_exped", "r_step", "r_read", "pay_copied",
                             "scattered"))
        with nc.Block() as block:
            @block.sync
            def _(sp):
                sp.dma_start(wr[:, :, :], w_router.rearrange("(k p) n -> p k n", p=P)).then_inc(w_loaded, 16)
                with sp.Fori(0, chunks // 2) as t:
                    for i in range(2):
                        c = 2 * t + i
                        hold(sp, o_turned, TC * c, sp_passed)
                        sp.dma_start(o_in[i][:, :, :], o_rows[:, :, bass.ds((c0 + c) * CH, CH)].rearrange("g p n -> p g n")
                                     ).then_inc(o_loaded[i], 16)

            @block.gpsimd
            def _(pool):
                if half == 1:
                    scatter_rows(pool, SENT_AFTER, pay, slots, x_rows, scattered)
                    pool.wait_ge(scattered, 16 * len(SENT_AFTER) * TOPK)

            @block.scalar
            def _(act):
                with act.Fori(0, chunks) as c:
                    sqrt_chunk(act, norm_step, NORM_STEPS * c, rstd)
                    act.wait_ge(norm_step, NORM_STEPS * (c + 1))
                    act.activation(pay[:, bass.ds((c0 + c) * TC, TC), 0:D], h[:, :, :], ACT.Copy).then_inc(pay_copied, 1)
                    act.wait_ge(r_summed, c)
                    for k in range(KD):
                        act.wait_ge(hT_summed, KD * c + k + 1)
                        act.activation(hT[:, k, :], psT[k][:, :], ACT.Copy).then_inc(hT_copied, 1)
                    act.wait_ge(r_summed, c + 1)
                    act.wait_ge(r_read, c)
                    act.activation(r_exp[:, :, :], psR[:, :, :], ACT.Exp, scale=-1.0).then_inc(r_exped, 1)

            @block.vector
            def _(dve):
                XS, RS = TC + 2, 1

                def add_attention(c):
                    link = Chain(dve, x_step, XS * c)
                    for j in range(TC):
                        heads = psO[j][:, :].rearrange("p (h w) -> p h w", h=H0)
                        dve.wait_ge(o_turned, TC * (c + 1) + j + 1)
                        link(dve.reciprocal(rden[:, j, :], heads[:, :, HD0]))
                        dve.tensor_tensor(o_tok[:, j, :].rearrange("p (h d) -> p h d", h=H0), heads[:, :, 0:HD0],
                                          rden[:, j, :].unsqueeze(2).to_broadcast([P, H0, HD0]),
                                          ALU.mult).then_inc(o_read, 1)
                    dve.wait_ge(o_read, TC * (c + 1))
                    link(dve.tensor_tensor(o_tok[:, :, :], o_tok[:, :, :],
                                           mod[:, GA, :].unsqueeze(1).to_broadcast([P, TC, D]), ALU.mult))
                    tiles = xres[:, bass.ds((c0 + c) * TC, TC), :]
                    link(dve.tensor_tensor(tiles, tiles, o_tok[:, :, :], ALU.add))
                    assert link.n == XS

                def chunk(c, t, i, another):
                    tiles = bass.ds((c0 + c) * TC, TC)
                    dve.wait_ge(hT_summed, KD * c)
                    hold(dve, pay_copied, c, dve_passed)
                    norm_chunk(dve, norm_step, dve_passed, NORM_STEPS * c, xres[:, tiles, :], stats, aggr, rstd,
                               h, mod[:, CB, :], mod[:, SB, :])
                    if another:
                        add_attention(c + 1)
                    link = Chain(dve, r_step, RS * c)
                    dve.wait_ge(r_exped, c + 1)
                    link(dve.tensor_scalar_add(r_exp[:, :, :], r_exp[:, :, :], 1.0))
                    dve.reciprocal(scores[:, tiles, :], r_exp[:, :, :]).then_inc(r_read, 1)
                add_attention(0)
                chunk_pairs(chunk, chunks)(dve)

            @block.tensor
            def _(pe):
                pe.sem_inc(o_turned, TC)
                pe.wait_ge(w_loaded, 16)

                def turn_attention(c, t, i):
                    pe.wait_ge(o_loaded[i], 16 * (t + 1))
                    pe.wait_ge(o_read, TC * c)
                    for j in range(TC):
                        for g in range(NG):
                            mm = pe.transpose(psO[j][:, g * P:(g + 1) * P], o_in[i][:, g, j * P:(j + 1) * P],
                                              ident[:, :])
                        mm.then_inc(o_turned, 1)

                def chunk(c, t, i, another):
                    if another:
                        turn_attention(c + 1, t + i, 1 - i)
                    pe.wait_ge(norm_step, NORM_STEPS * (c + 1))
                    pe.wait_ge(hT_copied, KD * c)
                    for k in range(KD):
                        for j in range(TC):
                            mm = pe.transpose(psT[k][:, j * P:(j + 1) * P], h[:, j, k * P:(k + 1) * P], ident[:, :])
                        mm.then_inc(hT_summed, 1)
                    pe.wait_ge(hT_copied, KD * (c + 1))
                    pe.wait_ge(r_read, c)
                    for j in range(TC):
                        for k in range(KD):
                            mm = pe.matmul(psR[:, j, :], hT[:, k, j * P:(j + 1) * P], wr[:, k, :],
                                           start=(k == 0), stop=(k == KD - 1))
                    mm.then_inc(r_summed, 1)
                turn_attention(0, 0, 0)
                chunk_pairs(chunk, chunks)(pe)


def route(nc, half, pay_all, scores_all, slots_all, taken, e_bias, x_rows):
    with ExitStack() as ctx:
        sb = lambda n, s, d=F32: ctx.enter_context(nc.sbuf_tensor(f"route{half}_" + n, s, d))
        pb = lambda n, s, d=F32: ctx.enter_context(nc.psum_tensor(f"route{half}_" + n, s, d))
        sem = ctx.enter_context(fresh_semaphores(nc, f"route{half}_"))
        NH = NT // 2
        mine = slice(half * NH, (half + 1) * NH)
        pay, scores, slots = (a[:, mine, :] for a in (pay_all, scores_all, slots_all))
        NGT = NH * NGRP
        bias = sb("e_bias_wide", [P, E])
        biased, hi, lo = sb("biased", [P, NH, E]), sb("hi", [P, NGT, 4]), sb("lo", [P, NGT, 4])
        hi2, lo2, mid2 = sb("hi2", [P, NGT, 2]), sb("lo2", [P, NGT, 2]), sb("mid2", [P, NGT, 2])
        hi3, lo3, mid3 = sb("hi3", [P, NGT, 1]), sb("lo3", [P, NGT, 1]), sb("mid3", [P, NGT, 1])
        gsum = sb("gsum", [P, NH, NGRP])
        ahead, tied = sb("ahead", [P, NH, NGRP, NGRP]), sb("tied", [P, NH, NGRP, NGRP])
        below = sb("below", [P, NGRP, NGRP])
        rank = sb("rank", [P, NH, NGRP])
        open_, picked = (a[:, :, :, :].rearrange("p n g e -> p n (g e)") for a in (tied, ahead))
        best = sb("best", [P, NH, TOPK])
        mask = sb("mask", [P, NH, E])
        maskb = sb("maskb", [P, NH, E], BF16)
        wsum = sb("wsum", [P, NH])
        before, onesb = sb("before", [P, P], BF16), sb("onesb", [P, P], BF16)
        base = biased
        pos, fits = sb("pos", [P, NH, E]), open_
        first_row = sb("first_row", [P, E])
        spare = sb("spare", [P, 1])
        key8, none8 = sb("key8", [P, NH, TOPK]), sb("none8", [P, NH, TOPK])
        NBK = NH * E // CH
        psP = [pb(f"psP{b}", [P, CH // E, E]) for b in range(NBK)]
        psS = [pb(f"psS{b}", [P, CH // E, E]) for b in range(NBK)]
        bias_loaded, const_set, pool_step, step, mask_set, pos_summed, base_step, scattered = (
            sem(n) for n in ("bias_loaded", "const_set", "pool_step", "step", "mask_set", "pos_summed", "base_step",
                             "scattered"))
        with nc.Block() as block:
            @block.sync
            def _(sp):
                sp.dma_start(bias[:, :], e_bias.partition_broadcast(P)).then_inc(bias_loaded, 16)

            @block.gpsimd
            def _(pool):
                link = Chain(pool, pool_step)
                link(pool.memset(below[:, :, :], 0.0))
                pool.affine_select(out=below[:, :, :], in_=below[:, :, :], compare_op=ALU.is_ge, fill=1.0, base=0,
                                   pattern=[[-1, NGRP], [1, NGRP]], channel_multiplier=0).then_inc(const_set, 1)
                pool.memset(onesb[:, :], 1.0).then_inc(const_set, 1)
                link(pool.memset(before[:, :], 0.0))
                pool.affine_select(out=before[:, :], in_=before[:, :], compare_op=ALU.is_ge, fill=1.0, base=0,
                                   pattern=[[-1, P]], channel_multiplier=1).then_inc(const_set, 1)
                pool.iota(first_row[:, :], pattern=[[CAP, E]], base=1, channel_multiplier=0,
                          allow_small_or_imprecise_dtypes=True).then_inc(const_set, 1)
                pool.iota(spare[:, :], pattern=[[0, 1]], base=SLOTS + 1, channel_multiplier=1,
                          allow_small_or_imprecise_dtypes=True).then_inc(const_set, 1)
                if half == 1:
                    scatter_rows(pool, SENT_ROUTE, pay_all, slots_all, x_rows, scattered)
                    pool.wait_ge(scattered, 16 * len(SENT_ROUTE) * TOPK)

            @block.tensor
            def _(pe):
                pe.wait_ge(const_set, 5)
                pe.wait_ge(mask_set, 1)
                for ps, w in ((psP, before), (psS, onesb)):
                    for b in range(NBK):
                        mm = pe.matmul(ps[b][:, :, :], w[:, :], maskb[:, b * (CH // E):(b + 1) * (CH // E), :],
                                       start=True, stop=True)
                mm.then_inc(pos_summed, 1)

            @block.vector
            def _(dve):
                link = Chain(dve, step)
                every = lambda ap: ap.unsqueeze(1).to_broadcast([P, NH, E])
                dve.wait_ge(bias_loaded, 16)
                dve.wait_ge(const_set, 5)
                link(dve.tensor_tensor(biased[:, :, :], scores[:, :, :], every(bias[:, :]), ALU.add))
                v = biased[:, :, :].rearrange("p n (g e) -> p (n g) e", g=NGRP)
                dve.tensor_tensor(hi[:, :, :], v[:, :, 0:4], v[:, :, 4:8], ALU.max)
                link(dve.tensor_tensor(lo[:, :, :], v[:, :, 0:4], v[:, :, 4:8], ALU.min))
                for h0, l0, h1, m1, l1, n in ((hi, lo, hi2, mid2, lo2, 2), (hi2, lo2, hi3, mid3, lo3, 1)):
                    dve.tensor_tensor(h1[:, :, :], h0[:, :, 0:n], h0[:, :, n:2 * n], ALU.max)
                    dve.tensor_tensor(m1[:, :, :], h0[:, :, 0:n], h0[:, :, n:2 * n], ALU.min)
                    link(dve.tensor_tensor(l1[:, :, :], l0[:, :, 0:n], l0[:, :, n:2 * n], ALU.max))
                    link(dve.tensor_tensor(l1[:, :, :], l1[:, :, :], m1[:, :, :], ALU.max))
                link(dve.tensor_tensor(gsum[:, :, :].rearrange("p n (g a) -> p (n g) a", a=1), hi3[:, :, :], lo3[:, :, :],
                                       ALU.add))
                other = gsum[:, :, :].unsqueeze(2).to_broadcast([P, NH, NGRP, NGRP])
                own = gsum[:, :, :].unsqueeze(3).to_broadcast([P, NH, NGRP, NGRP])
                dve.tensor_tensor(ahead[:, :, :, :], other, own, ALU.is_gt)
                link(dve.tensor_tensor(tied[:, :, :, :], other, own, ALU.is_equal))
                link(dve.tensor_tensor(tied[:, :, :, :], tied[:, :, :, :],
                                       below[:, :, :].unsqueeze(1).to_broadcast([P, NH, NGRP, NGRP]), ALU.mult))
                link(dve.tensor_tensor(ahead[:, :, :, :], ahead[:, :, :, :], tied[:, :, :, :], ALU.add))
                link(dve.tensor_reduce(rank[:, :, :], ahead[:, :, :, :], AX, ALU.add))
                link(dve.tensor_scalar(rank[:, :, :], rank[:, :, :], float(TOPG), None, ALU.is_lt))
                link(dve.tensor_tensor(open_[:, :, :].rearrange("p n (g e) -> p n g e", g=NGRP),
                                       biased[:, :, :].rearrange("p n (g e) -> p n g e", g=NGRP),
                                       rank[:, :, :].unsqueeze(3).to_broadcast([P, NH, NGRP, GE]), ALU.mult))
                for n in range(NH):
                    last = dve.max(out=best[:, n, :], in_=open_[:, n, :])
                link(last)
                for n in range(NH):
                    last = dve.match_replace(out=picked[:, n, :], in_to_replace=best[:, n, :], in_values=open_[:, n, :],
                                             imm_value=TAKEN)
                link(last)
                dve.tensor_scalar(mask[:, :, :], picked[:, :, :], TAKEN, None, ALU.is_equal)
                dve.tensor_scalar(maskb[:, :, :], picked[:, :, :], TAKEN, None, ALU.is_equal).then_inc(mask_set, 1)
                dve.wait_ge(mask_set, 1)
                weights = pay[:, :, D:D + E]
                link(dve.tensor_tensor(weights, scores[:, :, :], mask[:, :, :], ALU.mult))
                link(dve.tensor_reduce(wsum[:, :], weights, AX, ALU.add))
                link(dve.tensor_scalar_add(wsum[:, :], wsum[:, :], 1e-20))
                link(dve.reciprocal(wsum[:, :], wsum[:, :]))
                link(dve.tensor_scalar_mul(wsum[:, :], wsum[:, :], ROUTE_SCALE))
                link(dve.tensor_tensor(weights, weights, wsum[:, :].unsqueeze(2).to_broadcast([P, NH, E]), ALU.mult))
                link(dve.tensor_copy(base[:, 0, :], taken[:, :]) if half else dve.memset(base[:, 0, :], 0.0))
                dve.wait_ge(pos_summed, 1)
                for n in range(1, NH):
                    link(dve.tensor_tensor(base[:, n, :], psS[(n - 1) * E // CH][:, (n - 1) % (CH // E), :],
                                           base[:, n - 1, :], ALU.add))
                link(dve.tensor_tensor(taken[:, :], psS[NBK - 1][:, CH // E - 1, :], base[:, NH - 1, :], ALU.add))
                for b in range(NBK):
                    part = slice(b * (CH // E), (b + 1) * (CH // E))
                    last = dve.tensor_tensor(pos[:, part, :], psP[b][:, :, :], base[:, part, :], ALU.add)
                link(last)
                link(dve.tensor_scalar(fits[:, :, :], pos[:, :, :], float(CAP), None, ALU.is_lt))
                link(dve.tensor_tensor(fits[:, :, :], fits[:, :, :], mask[:, :, :], ALU.mult))
                link(dve.tensor_tensor(pos[:, :, :], pos[:, :, :], every(first_row[:, :]), ALU.add))
                link(dve.tensor_tensor(pos[:, :, :], pos[:, :, :], fits[:, :, :], ALU.mult))
                for n in range(NH):
                    last = dve.max(out=key8[:, n, :], in_=pos[:, n, :])
                link(last)
                link(dve.tensor_scalar(none8[:, :, :], key8[:, :, :], 0.0, None, ALU.is_equal))
                link(dve.scalar_tensor_tensor(out=key8[:, :, :], in0=none8[:, :, :], scalar=spare[:, 0:1],
                                              in1=key8[:, :, :], op0=ALU.mult, op1=ALU.add))
                link(dve.tensor_scalar_add(slots[:, :, :], key8[:, :, :], -1.0))


def shared_expert(nc, xres, pay, slots, mod, ident, x_rows, w_gate, w_up, w_down):
    with ExitStack() as ctx:
        sb = lambda n, s, d=F32: ctx.enter_context(nc.sbuf_tensor("shr_" + n, s, d))
        pb = lambda n, s, d=F32: ctx.enter_context(nc.psum_tensor("shr_" + n, s, d))
        sem = ctx.enter_context(fresh_semaphores(nc, "shr_"))
        KF = FS // P
        wg, wu, wd = sb("wg", [P, KD, FS]), sb("wu", [P, KD, FS]), sb("wd", [P, KF, D])
        h = [sb(f"h{i}", [P, TC, D]) for i in range(2)]
        hT, gate, actT = sb("hT", [P, KD, CH]), sb("gate", [P, KF, CH]), sb("actT", [P, KF, CH])
        part = [sb(f"part{m}", [P, 2, D]) for m in range(2)]
        psT = [pb(f"psT{k}", [P, CH]) for k in range(KD)]
        psG, psU = ([pb(f"{n}{b}", [P, CH]) for b in range(KF)] for n in ("psG", "psU"))
        psD = [pb(f"psD{m}", [P, CH]) for m in range(2)]
        (w_loaded, scattered, h_copied, hT_summed, hT_copied, gu_summed, gated, act_done, down_summed, down_read, x_step) = (
            sem(n) for n in ("w_loaded", "scattered", "h_copied", "hT_summed", "hT_copied", "gu_summed", "gated",
                             "act_done", "down_summed", "down_read", "x_step"))
        with nc.Block() as block:
            @block.gpsimd
            def _(pool):
                scatter_rows(pool, SENT_SHARED, pay, slots, x_rows, scattered)
                pool.wait_ge(scattered, 16 * len(SENT_SHARED) * TOPK)

            @block.sync
            def _(sp):
                for w, src in ((wg, w_gate), (wu, w_up), (wd, w_down)):
                    sp.dma_start(w[:, :, :], src.rearrange("(k p) n -> p k n", p=P)).then_inc(w_loaded, 16)

            @block.scalar
            def _(act):
                with act.Fori(0, NC) as c:
                    act.wait_ge(gu_summed, KF * c)
                    for k in range(KD):
                        act.wait_ge(hT_summed, KD * c + k + 1)
                        act.activation(hT[:, k, :], psT[k][:, :], ACT.Copy).then_inc(hT_copied, 1)
                    for b in range(KF):
                        act.wait_ge(gu_summed, KF * c + b + 1)
                        act.wait_ge(act_done, KF * c)
                        act.activation(gate[:, b, :], psG[b][:, :], ACT.Silu).then_inc(gated, 1)

            @block.vector
            def _(dve):
                with dve.Fori(0, NC // 2) as t:
                    for i in range(2):
                        c = 2 * t + i
                        dve.tensor_copy(h[i][:, :, :], pay[:, bass.ds(c * TC, TC), 0:D]).then_inc(h_copied, 1)
                        dve.wait_ge(down_summed, 2 * c)
                        for b in range(KF):
                            dve.wait_ge(gated, KF * c + b + 1)
                            dve.tensor_tensor(actT[:, b, :], psU[b][:, :], gate[:, b, :], ALU.mult).then_inc(act_done, 1)
                        for m in range(2):
                            tiles = xres[:, bass.ds(c * TC + 2 * m, 2), :]
                            dve.wait_ge(down_summed, 2 * c + m + 1)
                            dve.tensor_tensor(part[m][:, :, :], psD[m][:, :].rearrange("p (n d) -> p n d", n=2),
                                              mod[:, GB, :].unsqueeze(1).to_broadcast([P, 2, D]),
                                              ALU.mult).then_inc(down_read, 1)
                            dve.wait_ge(down_read, 2 * c + m + 1)
                            dve.tensor_tensor(tiles, tiles, part[m][:, :, :], ALU.add).then_inc(x_step, 1)

            @block.tensor
            def _(pe):
                pe.wait_ge(w_loaded, 48)
                with pe.Fori(0, NC // 2) as t:
                    for i in range(2):
                        c = 2 * t + i
                        pe.wait_ge(h_copied, c + 1)
                        pe.wait_ge(hT_copied, KD * c)
                        for k in range(KD):
                            for j in range(TC):
                                mm = pe.transpose(psT[k][:, j * P:(j + 1) * P], h[i][:, j, k * P:(k + 1) * P], ident[:, :])
                            mm.then_inc(hT_summed, 1)
                        pe.wait_ge(hT_copied, KD * (c + 1))
                        pe.wait_ge(act_done, KF * c)
                        for b in range(KF):
                            for w, ps in ((wg, psG[b]), (wu, psU[b])):
                                for k in range(KD):
                                    mm = pe.matmul(ps[:, :], w[:, k, b * P:(b + 1) * P], hT[:, k, :],
                                                   start=(k == 0), stop=(k == KD - 1))
                            mm.then_inc(gu_summed, 1)
                        pe.wait_ge(act_done, KF * (c + 1))
                        pe.wait_ge(down_read, 2 * c)
                        for m in range(2):
                            for j in range(2):
                                for k in range(KF):
                                    mm = pe.matmul(psD[m][:, j * D:(j + 1) * D],
                                                   actT[:, k, (2 * m + j) * P:(2 * m + j + 1) * P], wd[:, k, :],
                                                   start=(k == 0), stop=(k == KF - 1))
                            mm.then_inc(down_summed, 1)


def experts(nc, ident, x_rows, y_rows, w13, w2t):
    with ExitStack() as ctx:
        sb = lambda n, s, d=F32: ctx.enter_context(nc.sbuf_tensor("exp_" + n, s, d))
        pb = lambda n, s, d=F32: ctx.enter_context(nc.psum_tensor("exp_" + n, s, d))
        sem = ctx.enter_context(fresh_semaphores(nc, "exp_"))
        CT = CAP // P
        w1w3 = [sb(f"w1w3{i}", [P, 2, KD, F]) for i in range(2)]
        w2 = [sb(f"w2{i}", [P, D]) for i in range(2)]
        x = [sb(f"x{i}", [P, CT, PAY]) for i in range(2)]
        xT = [sb(f"xT{i}", [P, KD, CAP]) for i in range(2)]
        wrow = [sb(f"wrow{i}", [P, CT]) for i in range(2)]
        gate = [sb(f"gate{i}", [P, CAP]) for i in range(2)]
        hidden = [sb(f"hidden{i}", [P, CAP]) for i in range(2)]
        y = [sb(f"y{i}", [P, CT, D]) for i in range(2)]
        psX = [pb(f"psX{i}", [P, KD, CAP]) for i in range(2)]
        psH = [pb(f"psH{i}", [P, CAP]) for i in range(2)]
        psU = [pb(f"psU{i}", [P, CAP]) for i in range(2)]
        psY = [pb(f"psY{i}", [P, CT, D]) for i in range(2)]
        w13_loaded, w2_loaded, x_loaded, y_stored = (
            [sem(f"{n}{i}") for i in range(2)] for n in ("w13_loaded", "w2_loaded", "x_loaded", "y_stored"))
        (sp_passed, dve_passed, xT_summed, xT_copied, h_summed, gated, h_done, y_summed, y_copied, w_picked) = (
            sem(n) for n in ("sp_passed", "dve_passed", "xT_summed", "xT_copied", "h_summed", "gated", "h_done",
                             "y_summed", "y_copied", "w_picked"))

        def run(eng, turn, first, last):
            turn(0, 0, 0)
            turn(1, 0, 1)
            first(0, 0, 0)
            with eng.Fori(0, E // 2 - 1) as t:
                turn(2 * t + 2, t + 1, 0)
                first(2 * t + 1, t, 1)
                last(2 * t, t, 0)
                turn(2 * t + 3, t + 1, 1)
                first(2 * t + 2, t + 1, 0)
                last(2 * t + 1, t, 1)
            first(E - 1, E // 2 - 1, 1)
            last(E - 2, E // 2 - 1, 0)
            last(E - 1, E // 2 - 1, 1)

        with nc.Block() as block:
            @block.sync
            def _(sp):
                def load_w13(e, i):
                    sp.dma_start(w1w3[i][:, :, :, :].rearrange("p m k f -> p (m k f)"),
                                 w13[bass.ds(e, 1)].rearrange("a p n -> p (a n)")).then_inc(w13_loaded[i], 16)

                def load_w2(e, i):
                    sp.dma_start(w2[i][:, :], w2t[bass.ds(e, 1)].rearrange("a f h -> f (a h)")).then_inc(w2_loaded[i], 16)

                def load_x(e, i):
                    sp.dma_start(x[i][:, :, :], x_rows[bass.ds(e * CAP, CAP), :].rearrange("(c p) d -> p c d", p=P)
                                 ).then_inc(x_loaded[i], 16)

                def iteration(e, i):
                    more = lambda d: not isinstance(e, int) or e + d < E
                    if more(4):
                        hold(sp, xT_summed, e + 3, sp_passed)
                        hold(sp, w_picked, e + 3, sp_passed)
                        load_x(e + 4, i)
                    if more(3):
                        hold(sp, h_summed, e + 2, sp_passed)
                        load_w13(e + 3, 1 - i)
                    if more(2):
                        hold(sp, y_summed, CT * (e + 1), sp_passed)
                        load_w2(e + 2, i)
                    hold(sp, y_copied, CT * (e + 2), sp_passed)
                    sp.dma_start(y_rows[bass.ds(e * CAP, CAP), :].rearrange("(c p) d -> p c d", p=P), y[i][:, :, :]
                                 ).then_inc(y_stored[i], 16)

                for i in range(2):
                    load_x(i, i)
                    load_w13(i, i)
                    load_w2(i, i)
                for i in range(2):
                    sp.wait_ge(xT_summed, i + 1)
                    sp.wait_ge(w_picked, i + 1)
                    load_x(2 + i, i)
                sp.wait_ge(h_summed, 1)
                load_w13(2, 0)
                with sp.Fori(0, E // 2 - 2) as t:
                    for i in range(2):
                        iteration(2 * t + i, i)
                for e in range(E - 4, E):
                    iteration(e, e % 2)
                for i in range(2):
                    sp.wait_ge(y_stored[i], 16 * E // 2)

            @block.scalar
            def _(act):
                def copy_x(e, t, i):
                    if not isinstance(e, int):
                        act.wait_ge(h_summed, e - 1)
                    act.wait_ge(xT_summed, e + 1)
                    act.activation(xT[i][:, :, :], psX[i][:, :, :], ACT.Copy).then_inc(xT_copied, 1)

                def silu(e, t, i):
                    act.wait_ge(h_summed, e + 1)
                    if not (isinstance(e, int) and e < 2):
                        act.wait_ge(h_done, e - 1)
                    act.activation(gate[i][:, :], psH[i][:, :], ACT.Silu).then_inc(gated, 1)
                run(act, copy_x, silu, lambda e, t, i: None)

            @block.vector
            def _(dve):
                dve.sem_inc(y_copied, CT)

                def pick(e, t, i):
                    dve.wait_ge(x_loaded[i], 16 * (t + 1))
                    if not isinstance(e, int):
                        dve.wait_ge(y_copied, CT * e)
                    dve.tensor_copy(wrow[i][:, :], x[i][:, :, bass.ds(D + e, 1)].rearrange("p c a -> p (c a)")
                                    ).then_inc(w_picked, 1)

                def multiply(e, t, i):
                    dve.wait_ge(gated, e + 1)
                    if not (isinstance(e, int) and e < 2):
                        dve.wait_ge(y_summed, CT * (e - 1))
                    dve.tensor_tensor(hidden[i][:, :], psU[i][:, :], gate[i][:, :], ALU.mult).then_inc(h_done, 1)

                def scale(e, t, i):
                    dve.wait_ge(w_picked, e + 1)
                    dve.wait_ge(y_stored[i], 16 * t)
                    dve.wait_ge(y_summed, CT * (e + 1))
                    for c in range(CT):
                        dve.tensor_scalar(y[i][:, c, :], psY[i][:, c, :], wrow[i][:, c:c + 1], None,
                                          ALU.mult).then_inc(y_copied, 1)
                pick(0, 0, 0)
                pick(1, 0, 1)
                multiply(0, 0, 0)
                with dve.Fori(0, E // 2 - 1) as t:
                    multiply(2 * t + 1, t, 1)
                    scale(2 * t, t, 0)
                    pick(2 * t + 2, t + 1, 0)
                    multiply(2 * t + 2, t + 1, 0)
                    scale(2 * t + 1, t, 1)
                    pick(2 * t + 3, t + 1, 1)
                multiply(E - 1, E // 2 - 1, 1)
                scale(E - 2, E // 2 - 1, 0)
                scale(E - 1, E // 2 - 1, 1)

            @block.tensor
            def _(pe):
                def turn(e, t, i):
                    pe.wait_ge(x_loaded[i], 16 * (t + 1))
                    if not isinstance(e, int):
                        pe.wait_ge(xT_copied, e - 1)
                    for c in range(CT):
                        for k in range(KD):
                            mm = pe.transpose(psX[i][:, k, c * P:(c + 1) * P], x[i][:, c, k * P:(k + 1) * P], ident[:, :])
                    mm.then_inc(xT_summed, 1)

                def first(e, t, i):
                    pe.wait_ge(w13_loaded[i], 16 * (t + 1))
                    pe.wait_ge(xT_copied, e + 1)
                    if not (isinstance(e, int) and e < 2):
                        pe.wait_ge(h_done, e - 1)
                    for m, ps in enumerate((psH[i], psU[i])):
                        for k in range(KD):
                            mm = pe.matmul(ps[:, :], w1w3[i][:, m, k, :], xT[i][:, k, :], start=(k == 0), stop=(k == KD - 1))
                    mm.then_inc(h_summed, 1)

                def last(e, t, i):
                    pe.wait_ge(w2_loaded[i], 16 * (t + 1))
                    pe.wait_ge(h_done, e + 1)
                    pe.wait_ge(y_copied, CT * e)
                    for c in range(CT):
                        mm = pe.matmul(psY[i][:, c, :], hidden[i][:, c * P:(c + 1) * P], w2[i][:, :], start=True, stop=True)
                        mm.then_inc(y_summed, 1)
                run(pe, turn, first, last)


H1 = 16
HD1 = D // H1
SCALE1 = 1.0 / 16.0
MASKED = -1e38
BLK = CH


def project_rope(nc, xres, slots, y_rows, mod_before, mod, ident, qT, kT, vals, w_blocks, cos_t, sin_t):
    with ExitStack() as ctx:
        sb = lambda n, s, d=F32: ctx.enter_context(nc.sbuf_tensor("rope_" + n, s, d))
        pb = lambda n, s, d=F32: ctx.enter_context(nc.psum_tensor("rope_" + n, s, d))
        sem = ctx.enter_context(fresh_semaphores(nc, "rope_"))
        w = sb("w", [P, 5, KD, P])
        cos, sin = sb("cos", [P, KD, CH]), sb("sin", [P, KD, CH])
        rows, total = ([sb(f"{n}{i}", s) for i in range(2)] for n, s in (("rows", [P, TOPK, D]), ("total", [P, D])))
        h = sb("h", [P, TC, D])
        h_head = sb("h_head", [P, TC, D])
        hT = sb("hT", [P, KD, CH])
        stats, aggr, rstd = sb("stats", [P, TC, 6]), sb("aggr", [P, TC, 2]), sb("rstd", [P, TC])
        turned = [sb(f"turned{i}", [P, CH]) for i in range(2)]
        psT = [pb(f"psT{k}", [P, CH]) for k in range(KD)]
        psA = [pb(f"psA{i}", [P, CH]) for i in range(2)]
        psB = [pb(f"psB{i}", [P, CH]) for i in range(2)]
        psV = [pb(f"psV{i}", [P, CH]) for i in range(2)]
        w_loaded = sem("w_loaded")
        t_loaded = sem("t_loaded")
        gathered = [sem(f"gathered{i}") for i in range(2)]
        rows_read, sum_step = sem("rows_read"), sem("sum_step")
        (norm_step, dve_passed, sp_passed, hT_summed, hT_copied, ab_summed, ab_read, rot_step, v_summed, v_copied) = (
            sem(n) for n in ("norm_step", "dve_passed", "sp_passed", "hT_summed", "hT_copied", "ab_summed", "ab_read",
                             "rot_step", "v_summed", "v_copied"))
        NAB = 2 * KD
        with nc.Block() as block:
            @block.sync
            def _(sp):
                sp.dma_start(w[:, :, :, :], w_blocks).then_inc(w_loaded, 16)
                with sp.Fori(0, NC) as c:
                    hold(sp, ab_read, NAB * (c + 1), sp_passed)
                    for buf, src in ((cos, cos_t), (sin, sin_t)):
                        sp.dma_start(buf[:, :, :], src[:, :, bass.ds(c * CH, CH)]).then_inc(t_loaded, 16)

            @block.gpsimd
            def _(pool):
                for n in range(NT):
                    if n >= 2:
                        pool.wait_ge(rows_read, n - 1)
                    for k in range(TOPK):
                        pool.indirect_dma_start(out=rows[n % 2][:, k, :], out_offset=None, in_=y_rows,
                                                in_offset=bass.IndirectOffsetOnAxis(
                                                    ap=slots[:, n, k:k + 1].bitcast(U32), axis=0)
                                                ).then_inc(gathered[n % 2], 16)

            @block.scalar
            def _(act):
                with act.Fori(0, NC) as c:
                    sqrt_chunk(act, norm_step, NORM_STEPS * c, rstd)
                    act.wait_ge(v_summed, 2 * c)
                    for k in range(KD):
                        act.wait_ge(hT_summed, KD * c + k + 1)
                        act.activation(hT[:, k, :], psT[k][:, :], ACT.Copy).then_inc(hT_copied, 1)
                    for m in range(2):
                        act.wait_ge(v_summed, 2 * c + m + 1)
                        act.activation(vals[:, bass.ds(c * TC + 2 * m, 2), :].rearrange("p n (d h) -> p n h d", h=H1),
                                       psV[m][:, :].rearrange("p (n h d) -> p n h d", n=2, h=H1),
                                       ACT.Copy).then_inc(v_copied, 1)

            @block.vector
            def _(dve):
                dve.sem_inc(ab_read, NAB)
                CS = 2

                def sum_rows(c, j):
                    n = TC * c + j
                    link = Chain(dve, sum_step, CS * n)
                    dve.wait_ge(gathered[j % 2], 16 * TOPK * (TC // 2 * c + j // 2 + 1))
                    dve.tensor_reduce(total[j % 2][:, :], rows[j % 2][:, :, :].rearrange("p k d -> p d k"), AX,
                                      ALU.add).then_inc(rows_read, 1)
                    dve.wait_ge(rows_read, n + 1)
                    link(dve.tensor_tensor(total[j % 2][:, :], total[j % 2][:, :], mod_before[:, GB, :], ALU.mult))
                    x = xres[:, bass.ds(n, 1), :].rearrange("p a d -> p (a d)")
                    link(dve.tensor_tensor(x, x, total[j % 2][:, :], ALU.add))

                def rotate(c, n):
                    b = n % KD
                    out = (qT, kT)[n // KD][:, b, bass.ds(c * CH, CH)]
                    dve.wait_ge(ab_summed, NAB * c + n + 1)
                    dve.tensor_tensor(turned[n % 2][:, :], psB[n % 2][:, :], sin[:, b, :], ALU.mult)
                    dve.tensor_tensor(out, psA[n % 2][:, :], cos[:, b, :], ALU.mult).then_inc(ab_read, 1)
                    dve.wait_ge(ab_read, NAB * (c + 1) + n + 1)
                    dve.tensor_tensor(out, out, turned[n % 2][:, :], ALU.add).then_inc(rot_step, 1)

                def chunk(c, another):
                    hold(dve, hT_summed, KD * c, dve_passed)
                    norm_chunk(dve, norm_step, dve_passed, NORM_STEPS * c, xres[:, bass.ds(c * TC, TC), :], stats,
                               aggr, rstd, h, mod[:, CA, :], mod[:, SA, :],
                               order=lambda ap: ap.rearrange("p n (q h) -> p n q h", h=H1),
                               out=h_head[:, :, :].rearrange("p n (h q) -> p n q h", h=H1))
                    if another:
                        sum_rows(c + 1, 0)
                        sum_rows(c + 1, 1)
                    dve.wait_ge(t_loaded, 32 * (c + 1))
                    for n in range(NAB):
                        rotate(c, n)
                    if another:
                        sum_rows(c + 1, 2)
                        sum_rows(c + 1, 3)
                for j in range(TC):
                    sum_rows(0, j)
                with dve.Fori(0, NC - 1) as c:
                    chunk(c, True)
                chunk(NC - 1, False)

            @block.tensor
            def _(pe):
                pe.wait_ge(w_loaded, 16)
                with pe.Fori(0, NC) as c:
                    pe.wait_ge(norm_step, NORM_STEPS * (c + 1))
                    pe.wait_ge(hT_copied, KD * c)
                    for b in range(KD):
                        for j in range(TC):
                            mm = pe.transpose(psT[b][:, j * P:(j + 1) * P], h_head[:, j, b * P:(b + 1) * P], ident[:, :])
                        mm.then_inc(hT_summed, 1)
                    pe.wait_ge(hT_copied, KD * (c + 1))
                    for n in range(NAB):
                        b, x = n % KD, n // KD
                        pe.wait_ge(ab_read, NAB * (c + 1) + n - 1)
                        pe.matmul(psA[n % 2][:, :], w[:, 2 * x, b, :], hT[:, b, :], start=True, stop=True)
                        pe.matmul(psB[n % 2][:, :], w[:, 2 * x + 1, b, :], hT[:, b, :], start=True,
                                  stop=True).then_inc(ab_summed, 1)
                    pe.wait_ge(v_copied, 2 * c)
                    for m in range(2):
                        for j in range(2):
                            for b in range(KD):
                                mm = pe.matmul(psV[m][:, j * D + b * P:j * D + (b + 1) * P],
                                               hT[:, b, (2 * m + j) * P:(2 * m + j + 1) * P], w[:, 4, b, :],
                                               start=True, stop=True)
                        mm.then_inc(v_summed, 1)


def causal_attention(nc, xres, mod, ident, qT, kT, vals):
    with ExitStack() as ctx:
        sb = lambda n, s, d=F32: ctx.enter_context(nc.sbuf_tensor("caus_" + n, s, d))
        pb = lambda n, s, d=F32: ctx.enter_context(nc.psum_tensor("caus_" + n, s, d))
        sem = ctx.enter_context(fresh_semaphores(nc, "caus_"))
        row = [sb(f"row{i}", [P, T]) for i in range(2)]
        mask = sb("mask", [P, TC, BLK])
        probT = [sb(f"probT{i}", [P, BLK]) for i in range(2)]
        top = [sb(f"top{i}", [P, 1]) for i in range(2)]
        den = [sb(f"den{i}", [P, 1]) for i in range(2)]
        part, most, rinv = sb("part", [P, T // BLK]), sb("most", [P, 1]), sb("rinv", [P, 1])
        o_sb = sb("o_sb", [P, D])
        psS = [pb(f"psS{i}", [P, BLK]) for i in range(3)]
        psT = [pb(f"psT{i}", [P, BLK]) for i in range(3)]
        psO = [pb(f"psO{i}", [P, D]) for i in range(2)]
        (mask_step, s_summed, s_copied, s_masked, top_ready, exped, t_turned, t_copied, o_summed, o_read, step) = (
            sem(n) for n in ("mask_step", "s_summed", "s_copied", "s_masked", "top_ready", "exped", "t_turned",
                             "t_copied", "o_summed", "o_read", "step"))
        blocks = lambda s: s // TC + 1
        before = lambda s: sum(blocks(n) for n in range(s))
        plain = lambda s: before(s) - s
        with nc.Block() as block:
            @block.gpsimd
            def _(pool):
                pool.memset(mask[:, :, :], 0.0).then_inc(mask_step, 1)
                pool.wait_ge(mask_step, 1)
                pool.affine_select(out=mask[:, :, :], in_=mask[:, :, :], compare_op=ALU.is_ge, fill=MASKED, base=0,
                                   pattern=[[P, TC], [-1, BLK]], channel_multiplier=1).then_inc(mask_step, 1)

            @block.tensor
            def _(pe):
                def scores(s):
                    for b in range(blocks(s)):
                        g = before(s) + b
                        if g >= 3:
                            last = [(t, m) for t in range(s + 1) for m in range(blocks(t)) if before(t) + m == g - 3][0]
                            if last[1] == blocks(last[0]) - 1:
                                pe.wait_ge(s_masked, last[0] + 1)
                            else:
                                pe.wait_ge(s_copied, plain(last[0]) + last[1] + 1)
                        for k in range(KD):
                            mm = pe.matmul(psS[g % 3][:, :], qT[:, k, s * P:(s + 1) * P], kT[:, k, b * BLK:(b + 1) * BLK],
                                           start=(k == 0), stop=(k == KD - 1))
                        mm.then_inc(s_summed, 1)

                def turn(s, b):
                    g = before(s) + b
                    if g >= 3:
                        pe.wait_ge(t_copied, g - 2)
                    for j in range(TC):
                        n = b * TC + j
                        mm = pe.transpose(psT[g % 3][:, j * P:(j + 1) * P], row[s % 2][:, n * P:(n + 1) * P], ident[:, :])
                    mm.then_inc(t_turned, 1)

                def products(s, b):
                    pe.wait_ge(t_copied, before(s) + b + 1)
                    for j in range(TC):
                        n = b * TC + j
                        mm = pe.matmul(psO[s % 2][:, :], probT[(before(s) + b) % 2][:, j * P:(j + 1) * P], vals[:, n, :],
                                       start=(n == 0), stop=(n == TC * blocks(s) - 1))
                    mm.then_inc(o_summed, 1)

                scores(0)
                for s in range(NT):
                    if s + 1 < NT:
                        scores(s + 1)
                    pe.wait_ge(exped, s + 1)
                    if s >= 2:
                        pe.wait_ge(o_read, s - 1)
                    turn(s, 0)
                    for b in range(blocks(s)):
                        if b + 1 < blocks(s):
                            turn(s, b + 1)
                        products(s, b)

            @block.scalar
            def _(act):
                def copies(s):
                    for b in range(blocks(s) - 1):
                        g = before(s) + b
                        act.wait_ge(s_summed, g + 1)
                        if b == 0 and s >= 2:
                            act.wait_ge(t_turned, before(s - 1))
                        act.activation(row[s % 2][:, b * BLK:(b + 1) * BLK], psS[g % 3][:, :], ACT.Copy).then_inc(s_copied, 1)

                def exps(s):
                    act.wait_ge(top_ready, s + 1)
                    if s >= 2:
                        act.wait_ge(o_read, s - 1)
                    width = blocks(s) * BLK
                    act.activation(row[s % 2][:, 0:width], row[s % 2][:, 0:width], ACT.Exp, bias=top[s % 2][:, 0:1],
                                   scale=SCALE1, accum_out=den[s % 2][:, 0:1]).then_inc(exped, 1)

                for s in range(NT):
                    copies(s)
                    exps(s)

            @block.vector
            def _(dve):
                link = Chain(dve, step)

                def maximum(s):
                    nb = blocks(s)
                    for b in range(nb - 1):
                        dve.wait_ge(s_copied, plain(s) + b + 1)
                        dve.tensor_reduce(part[:, b:b + 1], row[s % 2][:, b * BLK:(b + 1) * BLK], AX, ALU.max)
                    dve.wait_ge(s_summed, before(s + 1))
                    if s >= 2:
                        dve.wait_ge(t_turned, before(s - 1))
                        dve.wait_ge(exped, s - 1)
                    last = row[s % 2][:, (nb - 1) * BLK:nb * BLK]
                    dve.tensor_tensor(last, psS[(before(s) + nb - 1) % 3][:, :], mask[:, s % TC, :],
                                      ALU.add).then_inc(s_masked, 1)
                    dve.wait_ge(s_masked, s + 1)
                    link(dve.tensor_reduce(part[:, nb - 1:nb], last, AX, ALU.max))
                    link(dve.tensor_reduce(most[:, :], part[:, 0:nb], AX, ALU.max))
                    dve.tensor_scalar_mul(top[s % 2][:, :], most[:, :], -SCALE1).then_inc(top_ready, 1)

                dve.wait_ge(mask_step, 2)
                maximum(0)
                for s in range(NT):
                    if s + 1 < NT:
                        maximum(s + 1)
                    for b in range(blocks(s)):
                        g = before(s) + b
                        dve.wait_ge(t_turned, g + 1)
                        if g >= 2:
                            dve.wait_ge(o_summed, g - 1)
                        dve.tensor_copy(probT[g % 2][:, :], psT[g % 3][:, :]).then_inc(t_copied, 1)
                    link(dve.reciprocal(rinv[:, :], den[s % 2][:, :]))
                    dve.wait_ge(o_summed, before(s + 1))
                    dve.tensor_scalar(o_sb[:, :], psO[s % 2][:, :], rinv[:, 0:1], None, ALU.mult).then_inc(o_read, 1)
                    dve.wait_ge(o_read, s + 1)
                    link(dve.tensor_tensor(o_sb[:, :], o_sb[:, :], mod[:, GA, :], ALU.mult))
                    link(dve.tensor_tensor(xres[:, s, :], xres[:, s, :], o_sb[:, :], ALU.add))


def rope_tables():
    import numpy as np
    half = D // 2
    freq = (1.0 / 10000.0 ** (np.arange(half, dtype=np.float32) / np.float32(half))).astype(np.float32)
    angle = np.arange(T, dtype=np.float32)[:, None] * freq[None, :]
    pair = np.arange(D).reshape(HD1, H1).T.reshape(-1) // 2
    sign = np.where(np.arange(D).reshape(HD1, H1).T.reshape(-1) % 2 == 0, -1.0, 1.0).astype(np.float32)
    view = lambda a: np.ascontiguousarray(a.T.reshape(KD, P, T).transpose(1, 0, 2).astype(np.float32))
    return view(np.cos(angle)[:, pair]), view(np.sin(angle)[:, pair] * sign[None, :])


def rope_weights(w_q, w_k, w_v):
    import numpy as np
    out = np.zeros((P, 5, KD, P), w_q.dtype)
    swap = np.arange(H1) ^ 1
    for m, (w, cols) in enumerate(((w_q, None), (w_q, swap), (w_k, None), (w_k, swap), (w_v, None))):
        for h in range(H1):
            b, r = divmod(h, H1 // KD)
            to = r if cols is None else cols[h] % (H1 // KD)
            out[r * HD1:(r + 1) * HD1, m, b, to * HD1:(to + 1) * HD1] = w[:, :, h]
    return out


HL = 8
DK = 64
KDV = HL * DK
NE = 4
GC = P // 2
NPAIR = HL // 2
QSCALE = DK ** -0.5
GSCALE = 1.0 / 16.0
EPS1 = 1e-5
LORA, GLR = 64, 16
LOW_Q, LOW_K, LOW_GATE, LOW_G1, LOW_G2 = (0, 0), (0, 64), (1, 0), (1, 64), (1, 96)


def low_rank(nc, xres, mod, ident, hT_d, low_d, m2_d, emT_d, emask, erw, tri, cen, w_low, w_e):
    with ExitStack() as ctx:
        sb = lambda n, s, d=F32: ctx.enter_context(nc.sbuf_tensor("low_" + n, s, d))
        pb = lambda n, s, d=F32: ctx.enter_context(nc.psum_tensor("low_" + n, s, d))
        sem = ctx.enter_context(fresh_semaphores(nc, "low_"))
        w, we = sb("w", [P, KD, 2, P]), sb("we", [P, KD, NE])
        h = [sb(f"h{i}", [P, TC, D]) for i in range(2)]
        hT = [sb(f"hT{i}", [P, KD, CH]) for i in range(2)]
        low = [sb(f"low{i}", [P, 2, CH]) for i in range(2)]
        stats, aggr, rstd = sb("stats", [P, TC, 6]), sb("aggr", [P, TC, 2]), sb("rstd", [P, TC])
        logits = sb("logits", [P, NT, NE])
        probs, most, total = sb("probs", [P, NT, NE]), sb("most", [P, NT]), sb("total", [P, NT])
        free = sb("free", [P, NT])
        maskT = [sb(f"maskT{i}", [NE, CH]) for i in range(2)]
        m2 = [sb(f"m2{i}", [P, TC, 2, P]) for i in range(2)]
        psT = [pb(f"psT{k}", [P, CH]) for k in range(KD)]
        psL = [pb(f"psL{i}", [P, CH]) for i in range(2)]
        psE = pb("psE", [P, TC, NE])
        psM, psS = pb("psM", [P, CH]), pb("psS", [P, TC, P])
        w_loaded = sem("w_loaded")
        hT_stored, low_stored, m2_stored, mask_stored = (
            [sem(f"{n}{i}") for i in range(2)] for n in ("hT_stored", "low_stored", "m2_stored", "mask_stored"))
        (norm_step, dve_passed, sp_passed, hT_summed, hT_copied, low_summed, low_copied, e_summed, e_copied, tri_step,
         centered, exped, step, turned, tcopied, same_summed, same_masked) = (
            sem(n) for n in ("norm_step", "dve_passed", "sp_passed", "hT_summed", "hT_copied", "low_summed",
                             "low_copied", "e_summed", "e_copied", "tri_step", "centered", "exped", "step", "turned",
                             "tcopied", "same_summed", "same_masked"))
        with nc.Block() as block:
            @block.sync
            def _(sp):
                sp.dma_start(w[:, :, :, :], w_low).then_inc(w_loaded, 16)
                sp.dma_start(we[:, :, :], w_e.rearrange("(k p) n -> p k n", p=P)).then_inc(w_loaded, 16)
                with sp.Fori(0, NC // 2) as t:
                    for i in range(2):
                        c = 2 * t + i
                        hold(sp, hT_copied, KD * (c + 1), sp_passed)
                        sp.dma_start(hT_d[:, :, bass.ds(c * CH, CH)], hT[i][:, :, :]).then_inc(hT_stored[i], 16)
                        hold(sp, low_copied, 2 * (c + 1), sp_passed)
                        sp.dma_start(low_d[:, :, bass.ds(c * CH, CH)], low[i][:, :, :]).then_inc(low_stored[i], 16)
                for c in range(NC):
                    sp.wait_ge(tcopied, c + 1)
                    sp.dma_start(emT_d[:, c * CH:(c + 1) * CH], maskT[c % 2][:, :]).then_inc(mask_stored[c % 2], 16)
                    sp.wait_ge(same_masked, c + 1)
                    sp.dma_start(m2_d[:, c * TC:(c + 1) * TC, :, :], m2[c % 2][:, :, :, :]).then_inc(m2_stored[c % 2], 16)
                for i in range(2):
                    for done in (hT_stored, low_stored, m2_stored, mask_stored):
                        sp.wait_ge(done[i], 16 * NC // 2)

            @block.gpsimd
            def _(pool):
                pool.memset(tri[:, :], 1.0).then_inc(tri_step, 1)
                pool.memset(cen[:, :], 1.0).then_inc(tri_step, 1)
                pool.wait_ge(tri_step, 2)
                pool.affine_select(out=tri[:, :], in_=tri[:, :], compare_op=ALU.is_ge, fill=0.0, base=0,
                                   pattern=[[1, P]], channel_multiplier=-1).then_inc(tri_step, 1)
                pool.affine_select(out=cen[:, :], in_=cen[:, :], compare_op=ALU.is_ge, fill=0.0, base=GC - 1,
                                   pattern=[[0, P]], channel_multiplier=-1).then_inc(tri_step, 1)
                pool.wait_ge(tri_step, 4)
                pool.tensor_tensor(cen[:, :], tri[:, :], cen[:, :], ALU.subtract).then_inc(tri_step, 1)

            @block.scalar
            def _(act):
                def copies(c, t, i, another):
                    act.wait_ge(hT_stored[i], 16 * t)
                    for k in range(KD):
                        act.wait_ge(hT_summed, KD * (c + 1) + k + 1)
                        act.activation(hT[i][:, k, :], psT[k][:, :], ACT.Copy).then_inc(hT_copied, 1)
                    if another:
                        sqrt_chunk(act, norm_step, NORM_STEPS * (c + 1), rstd)
                    act.wait_ge(low_stored[i], 16 * t)
                    for m in range(2):
                        act.wait_ge(low_summed, 2 * c + m + 1)
                        act.activation(low[i][:, m, :], psL[m][:, :], ACT.Copy).then_inc(low_copied, 1)
                    act.wait_ge(e_summed, c + 1)
                    act.activation(logits[:, bass.ds(c * TC, TC), :], psE[:, :, :], ACT.Copy).then_inc(e_copied, 1)
                sqrt_chunk(act, norm_step, 0, rstd)
                chunk_pairs(copies)(act)
                act.wait_ge(centered, 1)
                act.activation(probs[:, :, :], probs[:, :, :], ACT.Exp).then_inc(exped, 1)
                for c in range(NC):
                    act.wait_ge(turned, c + 1)
                    if c >= 2:
                        act.wait_ge(mask_stored[c % 2], 16 * (c // 2))
                    act.activation(maskT[c % 2][:, :], psM[0:NE, :], ACT.Copy).then_inc(tcopied, 1)

            @block.vector
            def _(dve):
                with dve.Fori(0, NC // 2) as t:
                    for i in range(2):
                        c = 2 * t + i
                        hold(dve, hT_summed, KD * c, dve_passed)
                        norm_chunk(dve, norm_step, dve_passed, NORM_STEPS * c, xres[:, bass.ds(c * TC, TC), :], stats,
                                   aggr, rstd, h[i], mod[:, CB, :], mod[:, SB, :])
                link = Chain(dve, step)
                wide = lambda ap: ap.unsqueeze(2).to_broadcast([P, NT, NE])
                dve.wait_ge(e_copied, NC)
                link(dve.tensor_reduce(most[:, :], logits[:, :, :], AX, ALU.max))
                dve.tensor_tensor(probs[:, :, :], logits[:, :, :], wide(most[:, :]), ALU.subtract).then_inc(centered, 1)
                dve.wait_ge(exped, 1)
                link(dve.tensor_reduce(total[:, :], probs[:, :, :], AX, ALU.add))
                link(dve.reciprocal(total[:, :], total[:, :]))
                link(dve.tensor_tensor(probs[:, :, :], probs[:, :, :], wide(total[:, :]), ALU.mult))
                link(dve.tensor_reduce(erw[:, :], probs[:, :, :], AX, ALU.max))
                link(dve.tensor_tensor(emask[:, :, :], probs[:, :, :], wide(erw[:, :]), ALU.is_equal))
                link(dve.tensor_scalar(free[:, :], emask[:, :, 0], -1.0, 1.0, ALU.mult, ALU.add))
                for e in range(1, NE):
                    link(dve.tensor_tensor(emask[:, :, e], emask[:, :, e], free[:, :], ALU.mult))
                    link(dve.tensor_tensor(free[:, :], free[:, :], emask[:, :, e], ALU.subtract))
                assert link.n == 14 - 1
                dve.wait_ge(tri_step, 5)
                for c in range(NC):
                    dve.wait_ge(same_summed, c + 1)
                    if c >= 2:
                        dve.wait_ge(m2_stored[c % 2], 16 * (c // 2))
                    for x, what in enumerate((tri, cen)):
                        last = dve.tensor_tensor(m2[c % 2][:, :, x, :], psS[:, :, :],
                                                 what[:, :].unsqueeze(1).to_broadcast([P, TC, P]), ALU.mult)
                    last.then_inc(same_masked, 1)

            @block.tensor
            def _(pe):
                pe.sem_inc(hT_summed, KD)
                pe.wait_ge(w_loaded, 32)
                with pe.Fori(0, NC // 2) as t:
                    for i in range(2):
                        c = 2 * t + i
                        pe.wait_ge(norm_step, NORM_STEPS * (c + 1))
                        pe.wait_ge(hT_copied, KD * c)
                        for k in range(KD):
                            for j in range(TC):
                                mm = pe.transpose(psT[k][:, j * P:(j + 1) * P], h[i][:, j, k * P:(k + 1) * P], ident[:, :])
                            mm.then_inc(hT_summed, 1)
                        pe.wait_ge(hT_copied, KD * (c + 1))
                        pe.wait_ge(low_copied, 2 * c)
                        for m in range(2):
                            for k in range(KD):
                                mm = pe.matmul(psL[m][:, :], w[:, k, m, :], hT[i][:, k, :], start=(k == 0), stop=(k == KD - 1))
                            mm.then_inc(low_summed, 1)
                        pe.wait_ge(e_copied, c)
                        for j in range(TC):
                            for k in range(KD):
                                mm = pe.matmul(psE[:, j, :], hT[i][:, k, j * P:(j + 1) * P], we[:, k, :],
                                               start=(k == 0), stop=(k == KD - 1))
                        mm.then_inc(e_summed, 1)
                pe.wait_ge(step, 13)
                for c in range(NC):
                    if c >= 1:
                        pe.wait_ge(tcopied, c)
                    for j in range(TC):
                        mm = pe.transpose(psM[0:NE, j * P:(j + 1) * P], emask[:, c * TC + j, :], ident[:, :])
                    mm.then_inc(turned, 1)
                    pe.wait_ge(tcopied, c + 1)
                    if c >= 1:
                        pe.wait_ge(same_masked, c)
                    for j in range(TC):
                        cols = maskT[c % 2][:, j * P:(j + 1) * P]
                        mm = pe.matmul(psS[:, j, :], cols, cols, start=True, stop=True)
                    mm.then_inc(same_summed, 1)


def linear_attention(nc, xres, mod, ident, hT_d, low_d, m2_d, emT_d, emask, erw, tri, cen, w_qkv, w_up, biases, norm_w, w_o, out):
    with ExitStack() as ctx:
        sb = lambda n, s, d=F32: ctx.enter_context(nc.sbuf_tensor("gla_" + n, s, d))
        pb = lambda n, s, d=F32: ctx.enter_context(nc.psum_tensor("gla_" + n, s, d))
        sem = ctx.enter_context(fresh_semaphores(nc, "gla_"))
        two = lambda n, s: [sb(f"{n}{i}", s) for i in range(2)]
        wqkv = sb("wqkv", [P, 3, KD, KDV])
        wup = sb("wup", [P, 2, KDV])
        wo = sb("wo", [P, NPAIR, D])
        bias = sb("bias", [P, 2, KDV])
        nw = sb("nw", [P, DK])
        hc, lc, m2c = two("hc", [P, KD, P]), two("lc", [P, 2, P]), two("m2c", [P, 2, P])
        halves = sb("halves", [P, 2])
        zb = sb("zb", [P, 3, KDV])
        lz = sb("lz", [P, 3, KDV])
        ls = two("ls", [P, 3, KDV])
        eg, egn = sb("eg", [P, 2, KDV]), sb("egn", [P, 2, KDV])
        kx, q2s = sb("kx", [P, HL, DK]), sb("q2s", [P, KDV])
        kmx, ksum = sb("kmx", [P, HL]), sb("ksum", [P, HL])
        rwq = sb("rwq", [P, NT])
        v, kg1, gs = two("v", [P, KDV]), two("kg1", [P, KDV]), two("gs", [P, KDV])
        qg1, kg2, qg2 = sb("qg1", [P, KDV]), sb("kg2", [P, KDV]), sb("qg2", [P, KDV])
        ke = two("ke", [P, NE, KDV])
        emr = two("emr", [P, NE, P])
        cme = two("cme", [P, NE, 2])
        ftT = sb("ftT", [P, 4, NPAIR, P])
        qeT = sb("qeT", [P, NPAIR, NE, P])
        a1, a2 = sb("a1", [P, HL, P]), sb("a2", [P, HL, P])
        s1_end, s2_end = sb("s1_end", [P, NPAIR, DK]), sb("s2_end", [P, NPAIR, NE, DK])
        s1_mid, s2_mid = sb("s1_mid", [P, NPAIR, 2, DK]), sb("s2_mid", [P, NPAIR, NE, 2, DK])
        NDEC = NPAIR * 2 * (1 + NE)
        dec = sb("dec", [P, NDEC])
        dec1 = dec[:, 0:NPAIR * 2].rearrange("p (a c) -> p a c", c=2)
        dec2 = dec[:, NPAIR * 2:].rearrange("p (a e c) -> p a e c", e=NE, c=2)
        sq, on = sb("sq", [P, HL, DK]), sb("on", [P, HL, DK])
        ms = sb("ms", [P, HL])
        oT = sb("oT", [P, NPAIR, P])
        ob = two("ob", [P, D])
        psP = pb("psP", [P, 2, KDV])
        psW = [pb(f"psW{i}", [P, CH]) for i in range(2)]
        psS2 = pb("psS2", [P, NPAIR, NE, DK])
        psS1 = pb("psS1", [P, CH])
        kv1 = psS1[:, 0:NPAIR * DK].rearrange("p (a d) -> p a d", d=DK)
        pdec = psS1[:, NPAIR * DK:NPAIR * DK + NDEC]
        pdec1 = pdec[:, 0:NPAIR * 2].rearrange("p (a c) -> p a c", c=2)
        pdec2 = pdec[:, NPAIR * 2:].rearrange("p (a e c) -> p a e c", e=NE, c=2)
        psO = pb("psO", [P, HL, DK])
        w_loaded = sem("w_loaded")
        loaded = [sem(f"loaded{i}") for i in range(2)]
        stored = [sem(f"stored{i}") for i in range(2)]
        (sp_passed, pool_passed, const_set, halves_step, projected, biased, gate_copied, lz_step, ls_ready, k_centered,
         k_exped, k_step, q2_scaled, v_copied, g_exped, sig_ready, dense_ready, sparse_ready, gate_ready, cme_ready,
         ke_ready, qe_ready, feats_turned, feats_copied, scores_summed, scores_masked, a_ready, dec_summed,
         dec_exped, kv_summed, kv_read, state_set, state_done, intra_inter, squared, ms_ready, rms_step, rms_ready, o_step, o_read,
         on_ready, o_turned, o_copied, y_summed, y_read, y_step, y_ready) = (
            sem(n) for n in (
                "sp_passed pool_passed const_set halves_step projected biased gate_copied lz_step ls_ready k_centered "
                "k_exped k_step q2_scaled v_copied g_exped sig_ready dense_ready sparse_ready gate_ready cme_ready "
                "ke_ready qe_ready feats_turned feats_copied scores_summed scores_masked a_ready "
                "dec_summed dec_exped kv_summed kv_read state_set state_done intra_inter squared ms_ready rms_step rms_ready "
                "o_step o_read on_ready o_turned o_copied y_summed y_read y_step y_ready").split())
        Z1, Z2, ZG, K2, Q2, V, G1, G2, K1, Q1 = range(10)
        NP = 10

        def run(eng, prologue, iteration, epilogue):
            prologue((0, 0, 0))
            for i in range(2):
                iteration((i + 1, (i + 1) // 2, 1 - i), (i, 0, i), None if i == 0 else (0, 0, 0))
            with eng.Fori(1, NT // 2 - 1) as t:
                iteration((2 * t + 1, t, 1), (2 * t, t, 0), (2 * t - 1, t - 1, 1))
                iteration((2 * t + 2, t + 1, 0), (2 * t + 1, t, 1), (2 * t, t, 0))
            n = NT - 2
            iteration((n + 1, n // 2, 1), (n, n // 2, 0), (n - 1, n // 2 - 1, 1))
            iteration(None, (n + 1, n // 2, 1), (n, n // 2, 0))
            epilogue((NT - 1, n // 2, 1))

        with nc.Block() as block:
            @block.sync
            def _(sp):
                for dst, src in ((wqkv[:, :, :, :], w_qkv), (wup[:, :, :], w_up),
                                 (wo[:, :, :], w_o.rearrange("(a p) d -> p a d", p=P)),
                                 (bias[:, 0, :], biases[0].partition_broadcast(P)),
                                 (bias[:, 1, :], biases[1].partition_broadcast(P)),
                                 (nw[:, :], norm_w.partition_broadcast(P))):
                    sp.dma_start(dst, src).then_inc(w_loaded, 16)

                def load(tile):
                    m, _, i = tile
                    sp.dma_start(hc[i][:, :, :], hT_d[:, :, bass.ds(m * P, P)]).then_inc(loaded[i], 16)
                    sp.dma_start(lc[i][:, :, :], low_d[:, :, bass.ds(m * P, P)]).then_inc(loaded[i], 16)
                    sp.dma_start(m2c[i][:, :, :], m2_d[:, bass.ds(m, 1), :, :].rearrange("p a x t -> p (a x) t")).then_inc(loaded[i], 16)
                    sp.dma_start(emr[i][:, :, :], emT_d[:, bass.ds(m * P, P)].partition_broadcast(P)).then_inc(loaded[i], 16)

                def store(tile):
                    m, _, i = tile
                    hold(sp, y_ready, m + 1, sp_passed)
                    sp.dma_start(out[bass.ds(m * P, P), :], ob[i][:, :]).then_inc(stored[i], 16)

                def iteration(nxt, cur, prv):
                    if nxt is not None and not (isinstance(cur[0], int) and cur[0] == NT - 2):
                        hold(sp, scores_masked, 4 * (cur[0] + 1), sp_passed)
                        hold(sp, qe_ready, cur[0] + 1, sp_passed)
                        load((cur[0] + 2, cur[1] + 1, cur[2]))
                    if prv is not None:
                        store(prv)

                load((0, 0, 0))
                load((1, 0, 1))
                run(sp, lambda tile: None, iteration, store)
                for i in range(2):
                    sp.wait_ge(stored[i], 16 * NT // 2)

            @block.gpsimd
            def _(pool):
                pool.memset(halves[:, :], 1.0).then_inc(halves_step, 1)
                pool.wait_ge(halves_step, 1)
                pool.affine_select(out=halves[:, 0:1], in_=halves[:, 0:1], compare_op=ALU.is_ge, fill=0.0, base=GC - 1,
                                   pattern=[[0, 1]], channel_multiplier=-1).then_inc(halves_step, 1)
                pool.affine_select(out=halves[:, 1:2], in_=halves[:, 1:2], compare_op=ALU.is_ge, fill=0.0, base=-GC,
                                   pattern=[[0, 1]], channel_multiplier=1).then_inc(halves_step, 1)
                pool.wait_ge(halves_step, 3)
                pool.tensor_scalar(rwq[:, :], erw[:, :], QSCALE, None, ALU.mult).then_inc(const_set, 1)

                def expert_mask(m):
                    return emask[:, bass.ds(m, 1), :].rearrange("p a e -> p (a e)")

                def queries(tile):
                    m, h, i = tile
                    hold(pool, feats_copied, 4 * m + 4, pool_passed)
                    hold(pool, loaded[i], 64 * (h + 1), pool_passed)
                    hold(pool, intra_inter, m, pool_passed)
                    for b in range(NPAIR):
                        last = pool.tensor_tensor(qeT[:, b, :, :], ftT[:, 3, b, :].unsqueeze(1).to_broadcast([P, NE, P]),
                                                  emr[i][:, :, :], ALU.mult)
                    last.then_inc(qe_ready, 1)

                def half_masks(tile):
                    m, _, i = tile
                    pool.tensor_tensor(cme[i][:, :, :], expert_mask(m).unsqueeze(2).to_broadcast([P, NE, 2]),
                                       halves[:, :].unsqueeze(1).to_broadcast([P, NE, 2]), ALU.mult).then_inc(cme_ready, 1)

                def add_scores(tile):
                    m, _, i = tile
                    hold(pool, scores_masked, 4 * m + 4, pool_passed)
                    pool.tensor_tensor(a1[:, :, :], a1[:, :, :], a2[:, :, :], ALU.add).then_inc(a_ready, 1)

                def keys(tile):
                    m, _, i = tile
                    hold(pool, sparse_ready, 2 * m + 1, pool_passed)
                    for e in range(NE):
                        last = pool.tensor_tensor(ke[i][:, e, :], kg2[:, :],
                                                  emask[:, bass.ds(m, 1), e].to_broadcast([P, KDV]), ALU.mult)
                    last.then_inc(ke_ready, 1)

                def prologue(tile):
                    half_masks(tile)
                    keys(tile)

                def iteration(nxt, cur, prv):
                    queries(cur)
                    if nxt is not None:
                        half_masks(nxt)
                    add_scores(cur)
                    if nxt is not None:
                        keys(nxt)

                run(pool, prologue, iteration, lambda tile: None)

            @block.scalar
            def _(act):
                def copy_feats(tile):
                    m, _, i = tile
                    for x in range(4):
                        act.wait_ge(feats_turned, 4 * m + x + 1)
                        act.activation(ftT[:, x, :, :].rearrange("p a t -> p (a t)"), psW[x % 2][:, :], ACT.Copy
                                       ).then_inc(feats_copied, 1)

                def log_sigmoids(tile):
                    m, _, i = tile
                    act.wait_ge(projected, NP * m + ZG + 1)
                    act.wait_ge(gate_ready, m)
                    act.activation(zb[:, 2, :], psP[:, 0, :], ACT.Copy).then_inc(gate_copied, 1)
                    act.wait_ge(gate_copied, m + 1)
                    act.wait_ge(biased, 2 * m + 2)
                    act.activation(lz[:, :, :], zb[:, :, :], ACT.Abs).then_inc(lz_step, 1)
                    act.wait_ge(lz_step, 3 * m + 1)
                    act.activation(lz[:, :, :], lz[:, :, :], ACT.Exp, scale=-1.0).then_inc(lz_step, 1)
                    act.wait_ge(lz_step, 3 * m + 2)
                    act.activation(lz[:, :, :], lz[:, :, :], ACT.Ln, bias=1.0).then_inc(lz_step, 1)

                def copy_o(tile):
                    m, _, i = tile
                    act.wait_ge(o_turned, m + 1)
                    act.activation(oT[:, :, :].rearrange("p a t -> p (a t)"), psW[1][:, :], ACT.Copy).then_inc(o_copied, 1)

                def q2_and_v(tile):
                    m, _, i = tile
                    act.wait_ge(const_set, 1)
                    act.wait_ge(sparse_ready, 2 * m)
                    act.wait_ge(projected, NP * m + Q2 + 1)
                    act.activation(q2s[:, :], psP[:, 0, :], ACT.Copy, scale=rwq[:, bass.ds(m, 1)]).then_inc(q2_scaled, 1)
                    act.wait_ge(projected, NP * m + V + 1)
                    act.activation(v[i][:, :], psP[:, 1, :], ACT.Copy).then_inc(v_copied, 1)

                def decays(tile):
                    m, _, i = tile
                    act.wait_ge(dec_summed, m + 1)
                    act.wait_ge(state_done, m + 1)
                    act.activation(dec[:, :], pdec, ACT.Exp, scale=GSCALE).then_inc(dec_exped, 1)

                def exps(tile):
                    m, _, i = tile
                    act.wait_ge(k_centered, m + 1)
                    act.activation(kx[:, :, :], kx[:, :, :], ACT.Exp).then_inc(k_exped, 1)
                    act.wait_ge(ls_ready, m + 1)
                    act.activation(ls[i][:, 2, :], ls[i][:, 2, :], ACT.Exp).then_inc(sig_ready, 1)
                    act.wait_ge(projected, NP * m + G2 + 1)
                    act.activation(eg[:, :, :], psP[:, :, :], ACT.Exp, scale=GSCALE).then_inc(g_exped, 1)
                    act.activation(egn[:, :, :], psP[:, :, :], ACT.Exp, scale=-GSCALE).then_inc(g_exped, 1)

                def square(tile):
                    m, _, i = tile
                    act.wait_ge(intra_inter, m + 1)
                    act.activation(sq[:, :, :], psO[:, :, :], ACT.Square).then_inc(squared, 1)

                def rms(tile):
                    m, _, i = tile
                    act.wait_ge(ms_ready, m + 1)
                    act.activation(ms[:, :], ms[:, :], ACT.Ln).then_inc(rms_step, 1)
                    act.wait_ge(rms_step, m + 1)
                    act.activation(ms[:, :], ms[:, :], ACT.Exp, scale=-0.5).then_inc(rms_ready, 1)

                def iteration(nxt, cur, prv):
                    copy_feats(cur)
                    if nxt is not None:
                        log_sigmoids(nxt)
                    if prv is not None:
                        rms(prv)
                    decays(cur)
                    if nxt is not None:
                        q2_and_v(nxt)
                    if prv is not None:
                        copy_o(prv)
                    if nxt is not None:
                        exps(nxt)
                    square(cur)

                def prologue(tile):
                    log_sigmoids(tile)
                    q2_and_v(tile)
                    exps(tile)

                def epilogue(tile):
                    rms(tile)
                    copy_o(tile)
                run(act, prologue, iteration, epilogue)

            @block.vector
            def _(dve):
                for state in (s1_end, s1_mid, s2_end, s2_mid):
                    last = dve.memset(state[:], 0.0)
                last.then_inc(state_done, 1)
                dve.wait_ge(w_loaded, 96)

                def mean_square(tile):
                    m, _, i = tile
                    dve.wait_ge(squared, m + 1)
                    dve.tensor_reduce(ms[:, :], sq[:, :, :], AX, ALU.add).then_inc(o_step, 1)
                    dve.wait_ge(o_step, m + 1)
                    dve.tensor_scalar(ms[:, :], ms[:, :], 1.0 / DK, EPS1, ALU.mult, ALU.add).then_inc(ms_ready, 1)

                def add_bias(tile):
                    m, _, i = tile
                    for x, item in enumerate((Z1, Z2)):
                        dve.wait_ge(projected, NP * m + item + 1)
                        dve.tensor_tensor(zb[:, x, :], psP[:, x, :], bias[:, x, :], ALU.add).then_inc(biased, 1)

                def gated(tile):
                    m, _, i = tile
                    dve.wait_ge(rms_ready, m + 1)
                    dve.wait_ge(o_turned, m)
                    dve.tensor_tensor(on[:, :, :], psO[:, :, :], ms[:, :].unsqueeze(2).to_broadcast([P, HL, DK]),
                                      ALU.mult).then_inc(o_read, 1)
                    dve.wait_ge(o_read, m + 1)
                    dve.tensor_tensor(on[:, :, :], on[:, :, :], gs[i][:, :].rearrange("p (h d) -> p h d", h=HL),
                                      ALU.mult).then_inc(on_ready, 1)

                def center(tile):
                    m, _, i = tile
                    keys = psP[:, 1, :].rearrange("p (h d) -> p h d", h=HL)
                    dve.wait_ge(projected, NP * m + K2 + 1)
                    dve.tensor_reduce(kmx[:, :], keys, AX, ALU.max).then_inc(k_step, 1)
                    dve.wait_ge(k_step, 5 * m + 1)
                    dve.tensor_tensor(kx[:, :, :], keys, kmx[:, :].unsqueeze(2).to_broadcast([P, HL, DK]),
                                      ALU.subtract).then_inc(k_centered, 1)

                def mask_scores(tile):
                    m, _, i = tile
                    for x in range(4):
                        dve.wait_ge(scores_summed, 4 * m + x + 1)
                        dst = (a1, a2)[x // 2][:, x % 2::2, :]
                        what = (tri[:, :], m2c[i][:, 0, :])[x // 2]
                        dve.tensor_tensor(dst, psW[(x + 1) % 2][:, :].rearrange("p (h t) -> p h t", h=4),
                                          what.unsqueeze(1).to_broadcast([P, 4, P]), ALU.mult).then_inc(scores_masked, 1)

                def log_sigmoid(tile):
                    m, _, i = tile
                    dve.wait_ge(lz_step, 3 * m + 3)
                    dve.scalar_tensor_tensor(out=ls[i][:, :, :], in0=zb[:, :, :], scalar=0.0, in1=lz[:, :, :],
                                             op0=ALU.min, op1=ALU.subtract).then_inc(ls_ready, 1)

                def output(tile):
                    m, h, i = tile
                    dve.wait_ge(y_summed, m + 1)
                    dve.wait_ge(stored[i], 16 * h)
                    dve.tensor_tensor(ob[i][:, :], psW[0][:, 0:D], mod[:, GB, :], ALU.mult).then_inc(y_read, 1)
                    dve.wait_ge(y_read, m + 1)
                    dve.tensor_tensor(ob[i][:, :], ob[i][:, :], xres[:, bass.ds(m, 1), :].rearrange("p a d -> p (a d)"),
                                      ALU.add).then_inc(y_ready, 1)

                def decay_states(tile):
                    m, _, i = tile
                    dve.wait_ge(dec_exped, m + 1)
                    dve.wait_ge(intra_inter, m)
                    dve.wait_ge(state_done, m + 1)
                    for x in range(2):
                        part = slice(x * DK, (x + 1) * DK)
                        dve.tensor_tensor(s1_mid[part, :, x, :], s1_end[part],
                                          dec1[part, :, 0].unsqueeze(2).to_broadcast([DK, NPAIR, DK]), ALU.mult)
                        last = dve.tensor_tensor(s2_mid[part, :, :, x, :], s2_end[part],
                                                 dec2[part, :, :, 0].unsqueeze(3).to_broadcast([DK, NPAIR, NE, DK]),
                                                 ALU.mult)
                    last.then_inc(state_set, 1)

                def add_to_states(tile):
                    m, _, i = tile
                    dve.wait_ge(kv_summed, m + 1)
                    dve.wait_ge(state_set, m + 1)
                    for x in range(2):
                        part = slice(x * DK, (x + 1) * DK)
                        dve.tensor_tensor(s1_end[part], kv1[part], s1_mid[part, :, x, :], ALU.add)
                        last = dve.tensor_tensor(s2_end[part], psS2[part], s2_mid[part, :, :, x, :], ALU.add)
                    last.then_inc(kv_read, 1)
                    dve.wait_ge(kv_read, m + 1)
                    dve.tensor_tensor(s1_end[:, :, :], s1_end[:, :, :],
                                      dec1[:, :, 1].unsqueeze(2).to_broadcast([P, NPAIR, DK]), ALU.mult)
                    dve.tensor_tensor(s2_end[:, :, :, :], s2_end[:, :, :, :],
                                      dec2[:, :, :, 1].unsqueeze(3).to_broadcast([P, NPAIR, NE, DK]), ALU.mult
                                      ).then_inc(state_done, 1)

                def scaled(tile):
                    m, _, i = tile
                    dve.wait_ge(k_exped, m + 1)
                    dve.tensor_reduce(ksum[:, :], kx[:, :, :], AX, ALU.add).then_inc(k_step, 1)
                    dve.wait_ge(k_step, 5 * m + 2)
                    dve.reciprocal(ksum[:, :], ksum[:, :]).then_inc(k_step, 1)
                    dve.wait_ge(k_step, 5 * m + 3)
                    dve.tensor_tensor(ksum[:, :], ksum[:, :], erw[:, bass.ds(m, 1)].to_broadcast([P, HL]),
                                      ALU.mult).then_inc(k_step, 1)
                    dve.wait_ge(k_step, 5 * m + 4)
                    dve.tensor_tensor(kx[:, :, :], kx[:, :, :], ksum[:, :].unsqueeze(2).to_broadcast([P, HL, DK]),
                                      ALU.mult).then_inc(k_step, 1)
                    dve.wait_ge(g_exped, 2 * m + 2)
                    dve.wait_ge(projected, NP * m + K1 + 1)
                    dve.tensor_tensor(kg1[i][:, :], psP[:, 0, :], egn[:, 0, :], ALU.mult).then_inc(dense_ready, 1)
                    dve.wait_ge(projected, NP * m + Q1 + 1)
                    dve.scalar_tensor_tensor(out=qg1[:, :], in0=psP[:, 1, :], scalar=QSCALE, in1=eg[:, 0, :],
                                             op0=ALU.mult, op1=ALU.mult).then_inc(dense_ready, 1)
                    dve.wait_ge(k_step, 5 * m + 5)
                    dve.wait_ge(ke_ready, m)
                    dve.wait_ge(feats_turned, 4 * m)
                    dve.tensor_tensor(kg2[:, :], kx[:, :, :].rearrange("p h d -> p (h d)"), egn[:, 1, :],
                                      ALU.mult).then_inc(sparse_ready, 1)
                    dve.wait_ge(q2_scaled, m + 1)
                    dve.tensor_tensor(qg2[:, :], q2s[:, :], eg[:, 1, :], ALU.mult).then_inc(sparse_ready, 1)
                    dve.wait_ge(sig_ready, m + 1)
                    dve.tensor_tensor(gs[i][:, :], zb[:, 2, :], ls[i][:, 2, :], ALU.mult).then_inc(y_step, 1)
                    dve.wait_ge(y_step, m + 1)
                    dve.tensor_tensor(gs[i][:, :].rearrange("p (h d) -> p h d", h=HL),
                                      gs[i][:, :].rearrange("p (h d) -> p h d", h=HL),
                                      nw[:, :].unsqueeze(1).to_broadcast([P, HL, DK]), ALU.mult).then_inc(gate_ready, 1)

                def iteration(nxt, cur, prv):
                    if prv is not None:
                        mean_square(prv)
                    if nxt is not None:
                        add_bias(nxt)
                    if nxt is not None:
                        center(nxt)
                    mask_scores(cur)
                    if prv is not None:
                        gated(prv)
                    if nxt is not None:
                        log_sigmoid(nxt)
                    decay_states(cur)
                    add_to_states(cur)
                    if prv is not None:
                        output(prv)
                    if nxt is not None:
                        scaled(nxt)

                def prologue(tile):
                    add_bias(tile)
                    center(tile)
                    log_sigmoid(tile)
                    scaled(tile)

                def epilogue(tile):
                    mean_square(tile)
                    gated(tile)
                    output(tile)
                run(dve, prologue, iteration, epilogue)

            @block.tensor
            def _(pe):
                pe.wait_ge(w_loaded, 96)

                def project(tile, item):
                    m, h, i = tile
                    ps = psP[:, item % 2, :]
                    if item == Z1:
                        pe.wait_ge(loaded[i], 64 * (h + 1))
                    semaphore, value = {
                        Z1: (dense_ready, 2 * m), Z2: (dense_ready, 2 * m), ZG: (biased, 2 * m + 1),
                        K2: (biased, 2 * m + 2), Q2: (gate_copied, m + 1), V: (k_centered, m + 1),
                        G1: (q2_scaled, m + 1), G2: (v_copied, m + 1), K1: (g_exped, 2 * m + 2),
                        Q1: (g_exped, 2 * m + 2)}[item]
                    pe.wait_ge(semaphore, value)
                    if item in (G1, G2):
                        if item == G1:
                            pe.wait_ge(ls_ready, m + 1)
                        x = item - G1
                        mm = pe.matmul(ps, (cen[:, :], m2c[i][:, 1, :])[x], ls[i][:, x, :], start=True, stop=True)
                    elif item in (Q1, K1, V):
                        x = {Q1: 0, K1: 1, V: 2}[item]
                        for k in range(KD):
                            mm = pe.matmul(ps, hc[i][:, k, :], wqkv[:, x, k, :], start=(k == 0), stop=(k == KD - 1))
                    else:
                        (b, r), rows = {Z1: (LOW_G1, GLR), Z2: (LOW_G2, GLR), ZG: (LOW_GATE, LORA), K2: (LOW_K, LORA),
                                        Q2: (LOW_Q, LORA)}[item]
                        mm = pe.matmul(ps, lc[i][r:r + rows, b, :], wup[r:r + rows, b, :], start=True, stop=True)
                    mm.then_inc(projected, 1)

                def turn_feats(tile):
                    m, _, i = tile
                    pe.wait_ge(dense_ready, 2 * m + 2)
                    for x, src in enumerate((kg1[i], qg1, kg2, qg2)):
                        if x < 2:
                            pe.wait_ge(scores_masked, 4 * m)
                            if not (isinstance(m, int) and m < 2):
                                pe.wait_ge((y_read, o_copied)[x], m - 1)
                        else:
                            pe.wait_ge(feats_copied, 4 * m + x - 1)
                            pe.wait_ge(sparse_ready, 2 * m + x - 1)
                        for b in range(NPAIR):
                            mm = pe.transpose(psW[x % 2][:, b * P:(b + 1) * P], src[:, b * P:(b + 1) * P], ident[:, :])
                        mm.then_inc(feats_turned, 1)

                def turn_o(tile, cur):
                    m, _, i = tile
                    pe.wait_ge(on_ready, m + 1)
                    if cur is not None:
                        pe.wait_ge(scores_masked, 4 * cur[0] + 3)
                    for b in range(NPAIR):
                        mm = pe.transpose(psW[1][:, b * P:(b + 1) * P],
                                          on[:, 2 * b:2 * b + 2, :].rearrange("p h d -> p (h d)"), ident[:, :])
                    mm.then_inc(o_turned, 1)

                def scores(tile):
                    m, _, i = tile
                    pe.wait_ge(feats_copied, 4 * m + 4)
                    for x in range(4):
                        if x >= 2:
                            pe.wait_ge(scores_masked, 4 * m + x - 1)
                        r = x % 2 * DK
                        for b in range(NPAIR):
                            mm = pe.matmul(psW[(x + 1) % 2][:, b * P:(b + 1) * P], ftT[r:r + DK, x // 2 * 2, b, :],
                                           ftT[r:r + DK, x // 2 * 2 + 1, b, :], start=True, stop=True)
                        mm.then_inc(scores_summed, 1)

                def project_o(tile, cur):
                    m, _, i = tile
                    pe.wait_ge(o_copied, m + 1)
                    if cur is not None:
                        pe.wait_ge(scores_masked, 4 * cur[0] + 4)
                    for b in range(NPAIR):
                        mm = pe.matmul(psW[0][:, 0:D], oT[:, b, :], wo[:, b, :], start=(b == 0), stop=(b == NPAIR - 1))
                    mm.then_inc(y_summed, 1)

                def decay_sums(tile):
                    m, _, i = tile
                    pe.wait_ge(kv_read, m)
                    pe.wait_ge(cme_ready, m + 1)
                    for b in range(NPAIR):
                        pe.matmul(pdec1[:, b, :], ls[i][:, 0, b * P:(b + 1) * P], halves[:, :], start=True, stop=True)
                    for b in range(NPAIR):
                        mm = pe.matmul(pdec2[:, b, :, :], ls[i][:, 1, b * P:(b + 1) * P], cme[i][:, :, :],
                                       start=True, stop=True)
                    mm.then_inc(dec_summed, 1)

                def keys_values(tile):
                    m, _, i = tile
                    pe.wait_ge(ke_ready, m + 1)
                    pe.wait_ge(dec_exped, m + 1)
                    for hh in range(HL):
                        head, rows = slice(hh * DK, (hh + 1) * DK), slice(hh % 2 * DK, hh % 2 * DK + DK)
                        for e in range(NE):
                            pe.matmul(psS2[rows, hh // 2, e, :], ke[i][:, e, head], v[i][:, head], start=True, stop=True)
                        mm = pe.matmul(kv1[rows, hh // 2, :], kg1[i][:, head], v[i][:, head], start=True, stop=True)
                    mm.then_inc(kv_summed, 1)

                def intra(tile):
                    m, _, i = tile
                    pe.wait_ge(a_ready, m + 1)
                    pe.wait_ge(v_copied, m + 1)
                    pe.wait_ge(o_read, m)
                    for hh in range(HL):
                        pe.matmul(psO[:, hh, :], a1[:, hh, :], v[i][:, hh * DK:(hh + 1) * DK],
                                  start=(hh == 0), stop=False, skip_group_check=True)

                def inter(tile):
                    m, _, i = tile
                    pe.wait_ge(state_set, m + 1)
                    pe.wait_ge(qe_ready, m + 1)
                    for b in range(NPAIR):
                        o = psO[:, 2 * b:2 * b + 2, :].rearrange("p h d -> p (h d)")
                        pe.matmul(o, ftT[:, 1, b, :], s1_mid[:, b, :, :].rearrange("p h d -> p (h d)"), start=False,
                                  stop=False, skip_group_check=True)
                        for e in range(NE):
                            mm = pe.matmul(o, qeT[:, b, e, :], s2_mid[:, b, e, :, :].rearrange("p h d -> p (h d)"),
                                           start=False, stop=(b == NPAIR - 1 and e == NE - 1), skip_group_check=True)
                    mm.then_inc(intra_inter, 1)

                def iteration(nxt, cur, prv):
                    ahead = lambda *items: [project(nxt, x) for x in items] if nxt is not None else None
                    ahead(Z1, Z2)
                    turn_feats(cur)
                    ahead(ZG, K2)
                    decay_sums(cur)
                    scores(cur)
                    ahead(Q2, V)
                    if prv is not None:
                        turn_o(prv, cur)
                    keys_values(cur)
                    if prv is not None:
                        project_o(prv, cur)
                    ahead(G1, G2)
                    intra(cur)
                    ahead(K1, Q1)
                    inter(cur)

                def prologue(tile):
                    for x in range(NP):
                        project(tile, x)

                def epilogue(tile):
                    turn_o(tile, None)
                    project_o(tile, None)
                run(pe, prologue, iteration, epilogue)


def program(nc, x, w_kqv, c0, wmod0, w_router, e_bias, w_gate, w_up, w_down, w13, w2t, c1, wmod1, w_rope, cos_t,
            sin_t, w_low, w_experts, w_qkv, w_lora_up, b_g1, b_g2, norm_w, w_o, k_aux, q_aux, out):
    dram = lambda name, shape, dt=F32: nc.dram_tensor(name, shape, dt).ap()
    with ExitStack() as whole:
        keep = lambda ctx, n, s, d=F32: ctx.enter_context(nc.sbuf_tensor(n, s, d))
        mod = [keep(whole, f"mod{l}", [P, 6, D]) for l in range(2)]
        ident, identb = keep(whole, "ident", [P, P]), keep(whole, "identb", [P, P], BF16)
        xres = keep(whole, "xres", [P, NT, D])
        modulation(nc, mod, ident, identb, [c0, c1], [wmod0, wmod1])

        q_parts, k_parts = (dram(n, (3, D, T), BF16) for n in ("q_parts", "k_parts"))
        v_aug = dram("v_aug", (NG, P, NT, P))
        o_rows = dram("o_rows", (NG, P, T))
        x_rows, y_rows = dram("x_rows", (SLOTS, PAY)), dram("y_rows", (SLOTS + SPARE, D))
        project_heads(nc, xres, mod[0], ident, x, w_kqv, q_parts, k_parts, v_aug)
        bias_attention(nc, identb, q_parts, k_parts, v_aug, k_aux.bitcast(BF16), q_aux.bitcast(BF16), o_rows,
                       x_rows, y_rows)

        slots = keep(whole, "slots", [P, NT, TOPK], I32)
        with ExitStack() as ctx:
            pay, scores = keep(ctx, "pay", [P, NT, PAY]), keep(ctx, "scores", [P, NT, E])
            taken = keep(ctx, "taken", [P, E])
            for half in range(2):
                after_attention(nc, half, xres, pay, slots, scores, mod[0], ident, o_rows, w_router, x_rows)
                route(nc, half, pay, scores, slots, taken, e_bias, x_rows)
            shared_expert(nc, xres, pay, slots, mod[0], ident, x_rows, w_gate, w_up, w_down)
        experts(nc, ident, x_rows, y_rows, w13, w2t)

        with ExitStack() as ctx:
            qT, kT, vals = keep(ctx, "qT", [P, KD, T]), keep(ctx, "kT", [P, KD, T]), keep(ctx, "vals", [P, NT, D])
            project_rope(nc, xres, slots, y_rows, mod[0], mod[1], ident, qT, kT, vals, w_rope, cos_t, sin_t)
            causal_attention(nc, xres, mod[1], ident, qT, kT, vals)

        hT_d, low_d = dram("hT_d", (P, KD, T)), dram("low_d", (P, 2, T))
        m2_d, emT_d = dram("m2_d", (P, NT, 2, P)), dram("emT_d", (NE, T))
        with ExitStack() as ctx:
            emask, erw = keep(ctx, "emask", [P, NT, NE]), keep(ctx, "erw", [P, NT])
            tri, cen = keep(ctx, "tri", [P, P]), keep(ctx, "cen", [P, P])
            low_rank(nc, xres, mod[1], ident, hT_d, low_d, m2_d, emT_d, emask, erw, tri, cen, w_low, w_experts)
            linear_attention(nc, xres, mod[1], ident, hT_d, low_d, m2_d, emT_d, emask, erw, tri, cen, w_qkv, w_lora_up,
                             [b_g1, b_g2], norm_w, w_o, out[0])


def expert_weights(w1, w3):
    import numpy as np
    by_row = np.stack([w.reshape(E, F, KD, P).transpose(0, 3, 2, 1) for w in (w1, w3)], axis=2)
    return by_row.reshape(E, P, 2 * KD * F)


def gla_weights(inputs):
    import numpy as np
    low, up = np.zeros((P, KD, 2, P), np.float32), np.zeros((P, 2, KDV), np.float32)
    for (b, r), down_name, up_name in ((LOW_Q, "Wqa", "Wqb"), (LOW_K, "Wka", "Wkb"), (LOW_GATE, "Wga", "Wgb"),
                                       (LOW_G1, "Wg1a", "Wg1b"), (LOW_G2, "Wg2a", "Wg2b")):
        a, u = np.asarray(inputs["L1_ffn_" + down_name]), np.asarray(inputs["L1_ffn_" + up_name])
        n = a.shape[1]
        low[:, :, b, r:r + n] = a.reshape(KD, P, n).transpose(1, 0, 2)
        up[r:r + n, b, :] = u
    qkv = np.stack([np.asarray(inputs["L1_ffn_" + n]).reshape(KD, P, KDV) for n in ("Wq", "Wk", "Wv")])
    return low, up, qkv.transpose(2, 0, 1, 3)


def kernel(**inputs):
    import numpy as np
    import concourse.bacc as bacc
    from concourse.bass_utils import run_bass_kernel_spmd

    get = lambda name: np.asarray(inputs[name])
    by_column = lambda c: c.reshape(KD, P).T
    low, up, qkv = gla_weights(inputs)
    cos_t, sin_t = rope_tables()
    k_aux, q_aux = bias_constants()
    laid_out = dict(
        x=get("L0_attn_x"), w_kqv=get("L0_attn_W_kqv"), c0=by_column(get("L0_c")), wmod0=get("L0_wmod"),
        w_router=get("L0_ffn_gate_weight").T, e_bias=get("L0_ffn_e_bias"), w_gate=get("L0_ffn_shared_gate").T,
        w_up=get("L0_ffn_shared_up").T, w_down=get("L0_ffn_shared_down").T, w13=expert_weights(get("L0_ffn_w1"), get("L0_ffn_w3")),
        w2t=get("L0_ffn_w2").transpose(0, 2, 1),
        c1=by_column(get("L1_c")), wmod1=get("L1_wmod"),
        w_rope=rope_weights(get("L1_attn_w_q"), get("L1_attn_w_k"), get("L1_attn_w_v")), cos_t=cos_t, sin_t=sin_t,
        w_low=low, w_experts=get("L1_ffn_We"), w_qkv=qkv, w_lora_up=up, b_g1=get("L1_ffn_bg1"),
        b_g2=get("L1_ffn_bg2"), norm_w=get("L1_ffn_norm_w"), w_o=get("L1_ffn_Wo"), k_aux=k_aux, q_aux=q_aux)

    nc = bacc.Bacc("TRN2", target_bir_lowering=False, num_devices=1)
    arrays, args = {}, {}
    for name, a in laid_out.items():
        arrays["in_" + name] = np.ascontiguousarray(a)
        args[name] = nc.dram_tensor("in_" + name, a.shape, mybir.dt.from_np(a.dtype), kind="ExternalInput").ap()
    out = nc.dram_tensor("out", (1, T, D), F32, kind="ExternalOutput").ap()
    program(nc, out=out, **args)
    r = run_bass_kernel_spmd(nc, [arrays], core_ids=[0])
    return r.results[0]["out"]
```
